# Optimizing a Trainium2 kernel written in Bass

```python
import numpy as np
import jax
import jax.numpy as jnp

def _softmax(x, axis=-1):
    return jax.nn.softmax(x, axis=axis)

def _gelu(x):
    return jax.nn.gelu(x, approximate=True)

def _silu(x):
    return jax.nn.silu(x)

def _sigmoid(x):
    return jax.nn.sigmoid(x)

def _layernorm(x, axis=-1, eps=1e-05):
    m = jnp.mean(x, axis=axis, keepdims=True)
    v = jnp.var(x, axis=axis, keepdims=True)
    return (x - m) / jnp.sqrt(v + eps)

def _scatter_add(tgt, idx, src, axis=0):
    return tgt.at[idx].add(src)

def _segment_sum(src, seg, n):
    return jax.ops.segment_sum(src, seg, n)
kernel_name = 'mk_adj_resnorm_d4_adj_r2_878009'

def setup_inputs(seed: int=0):
    np.random.seed(seed)
    _w = jnp.asarray

    def _rec_inputs():
        import jax
        import jax.numpy as jnp
        _gk = jax.random.key(seed)
        x = 7.22e-05 + 1 * jax.random.normal(jax.random.fold_in(_gk, 1), (64, 128, 256), jnp.float32)
        _w = (1.0 + jnp.arange(128, dtype=jnp.float32)) ** (-0.5)
        _w = _w / _w.mean()
        _pij = jnp.clip(0.125 * _w[:, None] * _w[None, :], 0.0, 1.0)
        _a = jax.random.uniform(jax.random.fold_in(_gk, 2), (64, 128, 128)) < _pij
        _a = jnp.logical_or(_a, jnp.swapaxes(_a, -1, -2))
        _a = jnp.logical_or(_a, jnp.eye(128, dtype=bool))
        _af = _a.astype(jnp.float32)
        _af = _af * jax.random.uniform(jax.random.fold_in(_gk, 3), (64, 128, 128), jnp.float32, 0.05, 1)
        adj = _af
        _nm = jnp.ones((64, 128), dtype=bool)
        nodemask = jnp.where(_nm, 1.0, 0.0).astype(jnp.float32)
        return (x, adj, nodemask)
    x, adj, nodemask = _rec_inputs()

    def _L0_gnn_setup():
        import jax, jax.numpy as jnp
        import numpy as np
        EPS_LN = 1e-05

        def hypergraph_conv(x, adj, W, b):
            N, C, _ = adj.shape
            H = (adj != 0).astype(x.dtype)
            w = adj.reshape(N, -1)[:, :C]
            xw = jnp.einsum('ncd,hd->nch', x, W)
            Dn = jnp.einsum('nce,ne->nc', H, w)
            Dn = jnp.where(Dn > 0, 1.0 / Dn, 0.0)
            Be = H.sum(axis=1)
            Be = jnp.where(Be > 0, 1.0 / Be, 0.0)
            m = Be[:, :, None] * jnp.einsum('nce,nch->neh', H, xw)
            out = Dn[:, :, None] * jnp.einsum('nce,neh->nch', H, m)
            return out + b

        def layer_norm(x, g, b):
            mu = jnp.mean(x, axis=-1, keepdims=True)
            var = jnp.var(x, axis=-1, keepdims=True)
            return (x - mu) * jax.lax.rsqrt(var + EPS_LN) * g + b
        key = jax.random.key(seed)
        ks = jax.random.split(key, 4)
        N, C, Din, Dh, Dout = (16, 512, 256, 512, 256)
        x = jax.random.normal(ks[0], (N, C, Din), dtype=jnp.float32)
        adj = jax.random.uniform(ks[1], (N, C, C), dtype=jnp.float32, minval=0.1, maxval=1.0)
        W1 = jax.random.normal(ks[2], (Dh, Din), dtype=jnp.float32) * (1.0 / np.sqrt(Din))
        b1 = jnp.zeros((Dh,), dtype=jnp.float32)
        gamma = jnp.ones((Dh,), dtype=jnp.float32)
        beta = jnp.zeros((Dh,), dtype=jnp.float32)
        W2 = jax.random.normal(ks[3], (Dout, Dh), dtype=jnp.float32) * (1.0 / np.sqrt(Dh))
        b2 = jnp.zeros((Dout,), dtype=jnp.float32)
        return {'x': x, 'adj': adj, 'W1': W1, 'b1': b1, 'gamma': gamma, 'beta': beta, 'W2': W2, 'b2': b2}
    _L0_gnn_all = _L0_gnn_setup()
    _L0_gnn_in = {k: v for k, v in _L0_gnn_all.items() if k in ('W1', 'b1', 'gamma', 'beta', 'W2', 'b2')}
    del _L0_gnn_all

    def _L1_gnn_setup():
        import jax, jax.numpy as jnp
        import numpy as np
        IN_F = 256
        OUT_F = 256
        ALPHA = 0.2
        NEG_INF = -9000000000000000.0
        key = jax.random.key(seed)
        k1, k2, k3, k4 = jax.random.split(key, 4)
        B, S = (8, 1024)
        hidden_state = jax.random.normal(k1, (B, S, IN_F), dtype=jnp.float32)
        adjacent_matrix = jax.random.uniform(k2, (B, S, S), dtype=jnp.float32)
        bound = 1.0 / np.sqrt(IN_F)
        W = jax.random.uniform(k3, (IN_F, OUT_F), dtype=jnp.float32, minval=-bound, maxval=bound)
        a_bound = 1.414 * np.sqrt(6.0 / (2 * OUT_F + 1))
        a = jax.random.uniform(k4, (2 * OUT_F, 1), dtype=jnp.float32, minval=-a_bound, maxval=a_bound)
        return {'hidden_state': hidden_state, 'adjacent_matrix': adjacent_matrix, 'W': W, 'a': a}
    _L1_gnn_all = _L1_gnn_setup()
    _L1_gnn_in = {k: v for k, v in _L1_gnn_all.items() if k in ('W', 'a')}
    del _L1_gnn_all

    def _L2_gnn_setup():
        import jax, jax.numpy as jnp
        import numpy as np
        B, N, DIN, DOUT = (8, 1024, 256, 256)
        EDGE_P = 0.01

        def _gcn_norm(adj):
            A = (adj != 0).astype(adj.dtype)
            eye = jnp.eye(A.shape[-1], dtype=A.dtype)
            A = jnp.maximum(A, eye)
            deg = A.sum(axis=-1)
            dinv = jnp.where(deg > 0, jax.lax.rsqrt(deg), 0.0)
            return dinv[..., :, None] * A * dinv[..., None, :]
        key = jax.random.key(seed)
        k1, k2, k3, k4 = jax.random.split(key, 4)
        inputs = jax.random.normal(k1, (B, N, DIN), dtype=jnp.float32)
        adj = (jax.random.uniform(k2, (B, N, N)) < EDGE_P).astype(jnp.float32)
        W = jax.random.normal(k3, (DIN, DOUT), dtype=jnp.float32) / np.sqrt(DIN)
        b = jax.random.normal(k4, (DOUT,), dtype=jnp.float32) * 0.01
        return {'inputs': inputs, 'adj': adj, 'W': W, 'b': b}
    _L2_gnn_all = _L2_gnn_setup()
    _L2_gnn_in = {k: v for k, v in _L2_gnn_all.items() if k in ('W', 'b')}
    del _L2_gnn_all

    def _L3_gnn_setup():
        import jax, jax.numpy as jnp
        import numpy as np
        B, N, IN_DIM, ATT_DIM = (2, 4096, 256, 256)
        key = jax.random.key(seed)
        k1, k2, k3, k4 = jax.random.split(key, 4)
        X = jax.random.normal(k1, (B, N, IN_DIM), dtype=jnp.float32)
        adj = jax.random.uniform(k2, (B, N, N), dtype=jnp.float32)
        mask = jnp.ones((B, N), dtype=jnp.float32)
        Wqk = jax.random.normal(k3, (IN_DIM, 2 * ATT_DIM), dtype=jnp.float32) / np.sqrt(IN_DIM)
        Wv = jax.random.normal(k4, (IN_DIM, IN_DIM), dtype=jnp.float32) / np.sqrt(IN_DIM)
        return {'X': X, 'adj': adj, 'mask': mask, 'Wqk': Wqk, 'Wv': Wv}
    _L3_gnn_all = _L3_gnn_setup()
    _L3_gnn_in = {k: v for k, v in _L3_gnn_all.items() if k in ('Wqk', 'Wv')}
    del _L3_gnn_all
    return {'x': x, 'adj': adj, 'nodemask': nodemask, 'L0_gnn_W1': _L0_gnn_in['W1'], 'L0_gnn_b1': _L0_gnn_in['b1'], 'L0_gnn_gamma': _L0_gnn_in['gamma'], 'L0_gnn_beta': _L0_gnn_in['beta'], 'L0_gnn_W2': _L0_gnn_in['W2'], 'L0_gnn_b2': _L0_gnn_in['b2'], 'L1_gnn_W': _L1_gnn_in['W'], 'L1_gnn_a': _L1_gnn_in['a'], 'L2_gnn_W': _L2_gnn_in['W'], 'L2_gnn_b': _L2_gnn_in['b'], 'L3_gnn_Wqk': _L3_gnn_in['Wqk'], 'L3_gnn_Wv': _L3_gnn_in['Wv']}

def reference(x, adj, nodemask, L0_gnn_W1, L0_gnn_b1, L0_gnn_gamma, L0_gnn_beta, L0_gnn_W2, L0_gnn_b2, L1_gnn_W, L1_gnn_a, L2_gnn_W, L2_gnn_b, L3_gnn_Wqk, L3_gnn_Wv):
    import jax
    import jax.numpy as jnp

    def _L0_gnn_ref(x, adj, W1, b1, gamma, beta, W2, b2):
        import jax, jax.numpy as jnp
        import numpy as np
        EPS_LN = 1e-05

        def hypergraph_conv(x, adj, W, b):
            N, C, _ = adj.shape
            H = (adj != 0).astype(x.dtype)
            w = adj.reshape(N, -1)[:, :C]
            xw = jnp.einsum('ncd,hd->nch', x, W)
            Dn = jnp.einsum('nce,ne->nc', H, w)
            Dn = jnp.where(Dn > 0, 1.0 / Dn, 0.0)
            Be = H.sum(axis=1)
            Be = jnp.where(Be > 0, 1.0 / Be, 0.0)
            m = Be[:, :, None] * jnp.einsum('nce,nch->neh', H, xw)
            out = Dn[:, :, None] * jnp.einsum('nce,neh->nch', H, m)
            return out + b

        def layer_norm(x, g, b):
            mu = jnp.mean(x, axis=-1, keepdims=True)
            var = jnp.var(x, axis=-1, keepdims=True)
            return (x - mu) * jax.lax.rsqrt(var + EPS_LN) * g + b
        h = jax.nn.relu(hypergraph_conv(x, adj, W1, b1))
        h = layer_norm(h, gamma, beta)
        y = hypergraph_conv(h, adj, W2, b2)
        return y + x

    def _L1_gnn_ref(hidden_state, adjacent_matrix, W, a):
        import jax, jax.numpy as jnp
        import numpy as np
        IN_F = 256
        OUT_F = 256
        ALPHA = 0.2
        NEG_INF = -9000000000000000.0
        Wh = jnp.einsum('bsi,io->bso', hidden_state, W)
        Wh1 = Wh @ a[:OUT_F, :]
        Wh2 = Wh @ a[OUT_F:, :]
        e = Wh1 + jnp.swapaxes(Wh2, 1, 2)
        e = jax.nn.leaky_relu(e, negative_slope=ALPHA)
        attention = jnp.where(adjacent_matrix > 0.5, e, NEG_INF)
        attention = jax.nn.softmax(attention, axis=1)
        h_prime = jnp.einsum('bst,bto->bso', attention, Wh)
        return jax.nn.elu(h_prime)

    def _L2_gnn_ref(inputs, adj, W, b):
        import jax, jax.numpy as jnp
        import numpy as np
        B, N, DIN, DOUT = (8, 1024, 256, 256)
        EDGE_P = 0.01

        def _gcn_norm(adj):
            A = (adj != 0).astype(adj.dtype)
            eye = jnp.eye(A.shape[-1], dtype=A.dtype)
            A = jnp.maximum(A, eye)
            deg = A.sum(axis=-1)
            dinv = jnp.where(deg > 0, jax.lax.rsqrt(deg), 0.0)
            return dinv[..., :, None] * A * dinv[..., None, :]
        norm = _gcn_norm(adj)
        h = jnp.einsum('bnf,fo->bno', inputs, W)
        agg = jnp.einsum('bnm,bmo->bno', norm, h)
        return jnp.tanh(agg + b)

    def _L3_gnn_ref(X, adj, mask, Wqk, Wv):
        import jax, jax.numpy as jnp
        import numpy as np
        B, N, IN_DIM, ATT_DIM = (2, 4096, 256, 256)
        qk = X @ Wqk
        q, k = jnp.split(qk, 2, axis=-1)
        v = X @ Wv
        att_dim = q.shape[-1]
        inv_scale = 1.0 / jnp.sqrt(jnp.float32(att_dim))
        k_m = k * mask[:, :, None]
        agg = jnp.einsum('bij,bjd->bid', adj, k_m)
        w = inv_scale * mask * jnp.einsum('bid,bid->bi', q, agg)
        L = jax.nn.softmax(w, axis=1)[:, :, None] * v
        return L
    x = _layernorm(x + _L0_gnn_ref(x, adj, L0_gnn_W1, L0_gnn_b1, L0_gnn_gamma, L0_gnn_beta, L0_gnn_W2, L0_gnn_b2), axis=-1)
    x = _layernorm(x + _L1_gnn_ref(x, adj, L1_gnn_W, L1_gnn_a), axis=-1)
    x = _layernorm(x + _L2_gnn_ref(x, adj, L2_gnn_W, L2_gnn_b), axis=-1)
    x = _layernorm(x + _L3_gnn_ref(x, adj, nodemask, L3_gnn_Wqk, L3_gnn_Wv), axis=-1)
    return x

_drawn_inputs = setup_inputs


def setup_inputs(seed=0):
    import zlib

    import numpy as np

    out = dict(_drawn_inputs(seed))
    spreads = {'L0_gnn_b1': (0.0, 0.1),
     'L0_gnn_gamma': (1.0, 0.2),
     'L0_gnn_beta': (0.0, 0.1),
     'L0_gnn_b2': (0.0, 0.1)}
    factors = {'L2_gnn_b': 8.0}
    for name, (base, spread) in spreads.items():
        noise = np.random.default_rng([zlib.crc32(name.encode()), seed]).standard_normal(out[name].shape)
        drawn = base * np.exp(spread * noise) if base else spread * noise
        out[name] = jnp.asarray(drawn.astype(out[name].dtype))
    for name, factor in factors.items():
        out[name] = (out[name] * factor).astype(out[name].dtype)
    return out
```

```python
import concourse.bass as bass
from concourse import mybir
from contextlib import ExitStack


def gnn_stack_kernel(
    nc: bass.Bass,
    x: bass.AP,
    adj: bass.AP,
    nodemask_t: bass.AP,
    w1_t: bass.AP,
    b1_cols: bass.AP,
    gamma_cols: bass.AP,
    beta_cols: bass.AP,
    w2_t: bass.AP,
    b2: bass.AP,
    gat_w: bass.AP,
    gat_w_t: bass.AP,
    gat_a_cols: bass.AP,
    gcn_w: bass.AP,
    gcn_b: bass.AP,
    wqk_t: bass.AP,
    wv: bass.AP,
    out: bass.AP,
):
    fp32 = mybir.dt.float32
    f32r = mybir.dt.float32r
    ALU = mybir.AluOpType
    ACT = mybir.ActivationFunctionType
    AX = mybir.AxisListType

    NGRAPH, N, D = x.shape
    DH = w1_t.shape[1]
    G = 4
    NG = NGRAPH // G
    KD = D // N
    KH = DH // N
    EPS = 1e-5
    NEG_INF = -9000000000000000.0
    SLOPE = 0.2
    SCALE = 1.0 / float(D) ** 0.5
    SQ = D + 4
    CONSTS = 16 * 15

    ctx = ExitStack()
    with ctx:
        def sb(name, shape, dt=fp32):
            return ctx.enter_context(nc.sbuf_tensor(name, shape, dt))

        def sem(name):
            return ctx.enter_context(nc.semaphore(name))

        ident = sb("ident", [N, N])
        mean_row = sb("mean_row", [N, N])
        neg_half = sb("neg_half", [N, G])
        nmask = sb("nmask", [N, NGRAPH])
        smask = sb("smask", [N, NGRAPH])
        no_loop = sb("no_loop", [N, NGRAPH])
        diag = sb("diag", [N, NGRAPH])
        b1_sb = sb("b1_sb", [N, KH])
        gamma_sb = sb("gamma_sb", [N, KH])
        beta_sb = sb("beta_sb", [N, KH])
        b2_row = sb("b2_row", [N, D])
        gcnb_row = sb("gcnb_row", [N, D])
        a_sb = sb("a_sb", [N, 2 * KD])
        beta_w2 = sb("beta_w2", [N, D])
        wa_row = sb("wa_row", [N, 2, D])
        W1 = [sb(f"w1_{s}", [N, KD, DH], f32r) for s in ("hi", "lo")]
        W2 = [sb(f"w2_{s}", [N, KH, D + 2], f32r) for s in ("hi", "lo")]
        WGAT = [sb(f"wgat_{s}", [N, KD, D], f32r) for s in ("hi", "lo")]
        WGCN = [sb(f"wgcn_{s}", [N, KD, D], f32r) for s in ("hi", "lo")]
        WUV = [sb(f"wuv_{s}", [N, KD, 2 * D], f32r) for s in ("hi", "lo")]

        adj_sb = sb("adj_sb", [N, 2, G, N])
        x_sb = sb("x_sb", [N, 2, G, D])
        wrow = sb("wrow", [N, 2, G, N])
        H = sb("H", [N, G, N])
        rowsum = sb("rowsum", [N, G])
        deg = sb("deg", [N, G])
        Dn = sb("Dn", [N, G])
        Dpos = sb("Dpos", [N, G])
        Dsafe = sb("Dsafe", [N, G])
        Drec = sb("Drec", [N, G])
        Dinv = sb("Dinv", [N, G])
        HD = sb("HD", [N, G, N])
        HT = sb("HT", [N, G, N])
        Be = sb("Be", [N, G])
        Bemax = sb("Bemax", [N, G])
        Binv = sb("Binv", [N, G])
        HTB = sb("HTB", [N, G, N])
        HDT = sb("HDT", [N, G, N])
        PT = sb("PT", [N, G, N])
        adjT = sb("adjT", [N, G, N])
        AT = sb("AT", [N, G, N])
        pxT = [sb(f"pxT_{s}", [N, KD, G, N], f32r) for s in ("hi", "lo")]
        r = sb("r", [N, KH, G, N])
        rT = [sb(f"rT_{s}", [N, KH, G, N], f32r) for s in ("hi", "lo")]
        sq = sb("sq", [N, KH, G, N])
        sqsum = sb("sqsum", [N, 2, G, N])
        hmean = sb("hmean", [N, G])
        hmean2 = sb("hmean2", [N, G])
        hvar = sb("hvar", [N, G])
        hvare = sb("hvare", [N, G])
        hrstd = sb("hrstd", [N, G])
        y = sb("y", [N, G, D])
        v0 = sb("v0", [N, G, D])
        negb = sb("negb", [N, 2, G, N])
        ATd = sb("ATd", [N, 2, G, N])
        adjTm = sb("adjTm", [N, 2, G, N])
        dinv = sb("dinv", [N, 2, G])

        x1 = sb("x1", [N, 2, G, D])
        wh = sb("wh", [N, 2, G])
        score = sb("score", [N, G, N])
        emax = sb("emax", [N, G])
        nemax = sb("nemax", [N, G])
        esum = sb("esum", [N, G])
        erec = sb("erec", [N, G])
        axT = [sb(f"axT_{s}", [N, KD, G, N], f32r) for s in ("hi", "lo")]
        hexp = sb("hexp", [N, G, D])
        v1 = sb("v1", [N, G, D])

        x2 = sb("x2", [N, 2, G, D])
        nxT = [sb(f"nxT_{s}", [N, KD, G, N], f32r) for s in ("hi", "lo")]
        v2 = sb("v2", [N, G, D])
        x3 = sb("x3", [N, 2, G, D])
        x3T = nxT
        z = sb("z", [N, G, D])
        wraw = sb("wraw", [N, G])
        wcol = sb("wcol", [N, G])
        vals = sb("vals", [N, G, D])

        wmax = sb("wmax", [G, 1])
        nwmax = sb("nwmax", [G, 1])
        pexp = sb("pexp", [G, N])
        psum_ = sb("psum_", [G, 1])
        prec = sb("prec", [G, 1])
        prow = sb("prow", [G, N])
        pcol = sb("pcol", [N, G])
        v3 = sb("v3", [N, G, D])
        x4 = sb("x4", [N, G, D])

        waste = H[:].rearrange("p g n -> p (g n)").rearrange("p (h d) -> p h d", h=2)

        def place(tile, chunks):
            return tile[:].rearrange("p g d -> p (g d)").rearrange("p (k n) -> p k n", k=chunks)

        raw_w1 = place(v3, KD)
        raw_w2 = place(vals, KH)
        w2g = place(v2, KH)
        raw_qk_t = place(z, 2 * KD)
        raw_uv = place(v1, KD)
        raw_gat, raw_gat_t = y[:, 0:2, :], y[:, 2:4, :]
        raw_gcn = hexp[:, 0:2, :]

        bn6 = sb("bn6", [N, 4, G, 6])
        mv = sb("mv", [N, 4, G, 2])
        vare = sb("vare", [N, 4, G])
        nmean = sb("nmean", [N, 4, G])
        rstd = sb("rstd", [N, 4, G])
        nmr = sb("nmr", [N, 4, G])

        ps = ctx.enter_context(nc.psum_tensor("ps", [N, 8, 512], fp32))

        def graphs(bank):
            return ps[:, bank, :].rearrange("p (g n) -> p g n", g=G)

        def halves(bank):
            return ps[:, bank, :].rearrange("p (g d) -> p g d", g=2)

        s_ident = sem("s_ident")
        s_w2g = sem("s_w2g")
        s_const = sem("s_const")
        s_prep_mm = sem("s_prep_mm")
        s_prep = sem("s_prep")
        s_loaded = [sem("s_loaded0"), sem("s_loaded1")]
        s_stored = sem("s_stored")
        s_HD = sem("s_HD")
        s_adjT = sem("s_adjT")
        s_adjTcp = sem("s_adjTcp")
        s_HT = sem("s_HT")
        s_AT = sem("s_AT")
        s_HTB = sem("s_HTB")
        s_HDTps = sem("s_HDTps")
        s_HDT = sem("s_HDT")
        s_Gps = sem("s_Gps")
        s_PT = sem("s_PT")
        s_px = sem("s_px")
        s_pxhi = sem("s_pxhi")
        s_pxlo = sem("s_pxlo")
        s_h = sem("s_h")
        s_r = sem("s_r")
        s_sq = sem("s_sq")
        s_rhl = sem("s_rhl")
        s_sqsum = sem("s_sqsum")
        s_ym = sem("s_ym")
        s_hvar = sem("s_hvar")
        s_hrstd = sem("s_hrstd")
        s_y = sem("s_y")
        s_py = sem("s_py")
        s_v0 = sem("s_v0")
        s_xb = sem("s_xb")
        s_sqfree = sem("s_sqfree")
        s_lnst = [sem(f"s_lnst{i}") for i in range(4)]
        s_lnrs = [sem(f"s_lnrs{i}") for i in range(4)]
        s_x1 = sem("s_x1")
        s_x2 = sem("s_x2")
        s_x3 = sem("s_x3")
        s_x4 = sem("s_x4")
        s_wh = sem("s_wh")
        s_bc = sem("s_bc")
        s_zb = sem("s_zb")
        s_el = sem("s_el")
        s_eexp = sem("s_eexp")
        s_att = sem("s_att")
        s_ax = sem("s_ax")
        s_axhi = sem("s_axhi")
        s_axlo = sem("s_axlo")
        s_hp = sem("s_hp")
        s_hexp = sem("s_hexp")
        s_hres = sem("s_hres")
        s_nx = sem("s_nx")
        s_nxhi = sem("s_nxhi")
        s_nxlo = sem("s_nxlo")
        s_agg = sem("s_agg")
        s_aggb = sem("s_aggb")
        s_th = sem("s_th")
        s_v2 = sem("s_v2")
        s_x3t = sem("s_x3t")
        s_x3hi = sem("s_x3hi")
        s_x3lo = sem("s_x3lo")
        s_z = sem("s_z")
        s_zcp = sem("s_zcp")
        s_uv = sem("s_uv")
        s_uz = sem("s_uz")
        s_v = sem("s_v")
        s_wcol = sem("s_wcol")
        s_wrow = sem("s_wrow")
        s_wmax = sem("s_wmax")
        s_pexp = sem("s_pexp")
        s_prow = sem("s_prow")
        s_pps = sem("s_pps")
        s_pcol = sem("s_pcol")
        s_ATd = sem("s_ATd")

        block = ctx.enter_context(nc.Block())

        def due(g, per, n):
            return g * per + n

        def before(eng, semaphore, g, per):
            if not (isinstance(g, int) and g == FIRST):
                eng.wait_ge(semaphore, g * per)

        FIRST, LAST = 0, NG - 1

        def schedule(eng, phase):
            def live(g):
                return g if 0 <= g < NG else None

            for n in range(4):
                phase(n % 2, live(n), live(n - 1), live(n - 2), live(n - 3))
            with eng.Fori(0, (NG - 6) // 2) as j:
                for u in range(2):
                    phase(u, 2 * j + 4 + u, 2 * j + 3 + u, 2 * j + 2 + u, 2 * j + 1 + u)
            for n in range(NG - 2, NG + 3):
                phase(n % 2, live(n), live(n - 1), live(n - 2), live(n - 3))

        @block.sync
        def _(sp):
            def load(g, q):
                sp.dma_start(adj_sb[:, q, :, :], adj[bass.ds(g * G, G), :, :].rearrange("g c e -> c g e")
                             ).then_inc(s_loaded[q], 16)
                sp.dma_start(wrow[:, q, :, :], adj[bass.ds(g * G, G), 0, :].unsqueeze(0).to_broadcast([N, G, N])
                             ).then_inc(s_loaded[q], 16)
                sp.dma_start(x_sb[:, q, :, :], x[bass.ds(g * G, G), :, :].rearrange("g n d -> n g d")
                             ).then_inc(s_loaded[q], 16)

            def rows(w):
                return w.rearrange("(k p) n -> p k n", p=N)

            load(0, 0)
            sp.dma_start(raw_w2, rows(w2_t)).then_inc(s_const, 16)
            sp.dma_start(diag[:], adj.rearrange("g n m -> g (n m)")[:, 0:N * N:N + 1].rearrange("g n -> n g"),
                         allow_slow_non_contiguous=True).then_inc(s_const, 16)
            sp.dma_start(nmask[:], nodemask_t).then_inc(s_const, 16)
            sp.dma_start(raw_w1, rows(w1_t)).then_inc(s_const, 16)
            sp.dma_start(b1_sb[:], b1_cols).then_inc(s_const, 16)
            sp.dma_start(gamma_sb[:], gamma_cols).then_inc(s_const, 16)
            sp.dma_start(beta_sb[:], beta_cols).then_inc(s_const, 16)
            sp.dma_start(b2_row[:], b2.unsqueeze(0).to_broadcast([N, D])).then_inc(s_const, 16)
            sp.dma_start(a_sb[:], gat_a_cols).then_inc(s_const, 16)
            sp.dma_start(raw_gat, rows(gat_w)).then_inc(s_const, 16)
            sp.dma_start(raw_gat_t, rows(gat_w_t)).then_inc(s_const, 16)
            sp.dma_start(raw_gcn, rows(gcn_w)).then_inc(s_const, 16)
            sp.dma_start(gcnb_row[:], gcn_b.unsqueeze(0).to_broadcast([N, D])).then_inc(s_const, 16)
            sp.dma_start(raw_qk_t, rows(wqk_t)).then_inc(s_const, 16)
            sp.dma_start(raw_uv[:, :, D:2 * D], rows(wv)).then_inc(s_const, 16)
            load(1, 1)

            def phase(p, a, b, c, t):
                if a is not None and b is not None and not (isinstance(a, int) and a == LAST):
                    sp.wait_ge(s_adjT, due(b, 1, 1))
                    sp.wait_ge(s_HD, due(b, 1, 1))
                    sp.wait_ge(s_px, due(b, KD, KD))
                    sp.wait_ge(s_xb, due(b, 1, 1))
                    load(a + 1, 1 - p)
                if t is not None:
                    sp.wait_ge(s_x4, due(t, 1, 1))
                    sp.dma_start(out[bass.ds(t * G, G), :, :].rearrange("g n d -> n g d"),
                                 x4[:]).then_inc(s_stored, 16)

            schedule(sp, phase)
            sp.wait_ge(s_stored, 16 * NG)

        @block.tensor
        def _(pe):
            mm = nc.tensor.matmul

            pe.wait_ge(s_const, CONSTS)
            pe.wait_ge(s_ident, 1)
            pe.wait_ge(s_w2g, 1)
            for k in range(KH):
                mm(ps[:, 0, 0:D], mean_row[:], w2g[:, k, :], start=k == 0, stop=k == KH - 1)
            for k in range(KH):
                mm(ps[:, 1, 0:D], beta_sb[:, k:k + 1].to_broadcast([N, N]), raw_w2[:, k, :],
                   start=k == 0, stop=k == KH - 1)
            for half in range(2):
                for k in range(KD):
                    mm(ps[:, 2, half * D:(half + 1) * D],
                       a_sb[:, half * KD + k:half * KD + k + 1].to_broadcast([N, N]), raw_gat_t[:, k, :],
                       start=k == 0, stop=k == KD - 1)
            for m in range(KD):
                for k in range(KD):
                    last = mm(ps[:, 3 + m, 0:D], raw_qk_t[:, k, m * N:(m + 1) * N], raw_qk_t[:, KD + k, :],
                              start=k == 0, stop=k == KD - 1)
            last.then_inc(s_prep_mm, 1)
            pe.wait_ge(s_prep, 1)

            def split_product(dst, left, right, chunks):
                for k in range(chunks):
                    for n, (s, w) in enumerate(((0, 0), (0, 1), (1, 0))):
                        last = mm(dst, left(s, k), right(w, k), start=k == 0 and n == 0,
                                  stop=k == chunks - 1 and n == 2)
                return last

            def feature_chunk(k):
                return slice(k * N, (k + 1) * N)

            def phase(p, a, b, c, t):
                if a is not None:
                    pe.wait_ge(s_loaded[p], 24 * (a - p) + 48)
                    before(pe, s_v0, a, 2)
                    for g in range(G):
                        last = nc.tensor.transpose(graphs(0)[:, g, :], adj_sb[:, p, g, :], ident[:])
                    last.then_inc(s_adjT, 1)
                if c is not None:
                    pe.wait_ge(s_x2, due(c, 1, 1))
                    pe.wait_ge(s_ATd, due(c, 1, 1))
                    before(pe, s_uz, c, G)
                    before(pe, s_v, c, G)
                    for k in range(KD):
                        for g in range(G):
                            last = mm(graphs(6 + k)[:, g, :], x2[:, p, g, feature_chunk(k)], ATd[:, p, g, :],
                                      start=True, stop=True)
                        last.then_inc(s_nx, 1)
                if a is not None:
                    pe.wait_ge(s_HD, due(a, 1, 1))
                    for g in range(G):
                        last = nc.tensor.transpose(graphs(1)[:, g, :], HD[:, g, :], ident[:])
                    last.then_inc(s_HDTps, 1)
                if c is not None:
                    pe.wait_ge(s_nxhi, due(c, KD, KD))
                    pe.wait_ge(s_nxlo, due(c, KD, KD))
                    for g in range(G):
                        last = split_product(halves(6 + g // 2)[:, g % 2, :],
                                             lambda s, k: nxT[s][:, k, g, :], lambda w, k: WGCN[w][:, k, :], KD)
                        if g % 2:
                            last.then_inc(s_agg, 1)
                if t is not None:
                    pe.wait_ge(s_wcol, due(t, 1, 1))
                    if b is not None:
                        before(pe, s_hexp, b, 2)
                        before(pe, s_hres, b, 2)
                    mm(ps[0:G, 5, 0:N], wcol[:], ident[:], start=True, stop=True).then_inc(s_wrow, 1)
                if a is not None:
                    pe.wait_ge(s_HTB, due(a, 1, 1))
                    pe.wait_ge(s_HDT, due(a, 1, 1))
                    for g in range(G):
                        last = mm(graphs(2)[:, g, :], HTB[:, g, :], HDT[:, g, :], start=True, stop=True)
                    last.then_inc(s_Gps, 1)
                if b is not None:
                    pe.wait_ge(s_wh, due(b, 1, 1))
                    before(pe, s_hexp, b, 2)
                    before(pe, s_hres, b, 2)
                    for g in range(G):
                        last = mm(graphs(4)[:, g, :], wh[:, 0, g:g + 1].to_broadcast([N, N]), ident[:],
                                  start=True, stop=True)
                    last.then_inc(s_bc, 1)
                if a is not None:
                    pe.wait_ge(s_PT, due(a, 1, 1))
                    for k in range(KD):
                        for g in range(G):
                            last = mm(graphs((3 + k) % 4)[:, g, :], x_sb[:, p, g, feature_chunk(k)], PT[:, g, :],
                                      start=True, stop=True)
                        last.then_inc(s_px, 1)
                if t is not None:
                    pe.wait_ge(s_prow, due(t, 1, 1))
                    mm(ps[:, 5, N:N + G], prow[:], ident[0:G, 0:G], start=True, stop=True).then_inc(s_pps, 1)
                if a is not None:
                    pe.wait_ge(s_pxhi, due(a, KD, KD))
                    pe.wait_ge(s_pxlo, due(a, KD, KD))
                    for h in range(KH):
                        split_product(ps[:, (1 + h) % 4, :],
                                      lambda s, k: W1[s][:, k, feature_chunk(h)],
                                      lambda w, k: pxT[w][:, k, :, :].rearrange("p g n -> p (g n)"), KD
                                      ).then_inc(s_h, 1)
                if b is not None:
                    pe.wait_ge(s_att, due(b, 1, 1))
                    if t is not None:
                        pe.wait_ge(s_pcol, due(t, 1, 1))
                    for k in range(KD):
                        for g in range(G):
                            last = mm(graphs(5 - k)[:, g, :], x1[:, 1 - p, g, feature_chunk(k)], score[:, g, :],
                                      start=True, stop=True)
                        last.then_inc(s_ax, 1)
                    pe.wait_ge(s_axhi, due(b, KD, KD))
                    pe.wait_ge(s_axlo, due(b, KD, KD))
                    for g in range(G):
                        last = split_product(halves(4 + g // 2)[:, g % 2, :],
                                             lambda s, k: axT[s][:, k, g, :], lambda w, k: WGAT[w][:, k, :], KD)
                        if g % 2:
                            last.then_inc(s_hp, 1)
                if c is not None:
                    pe.wait_ge(s_x3, due(c, 1, 1))
                    for k in range(KD):
                        for g in range(G):
                            last = nc.tensor.transpose(graphs(6 + k)[:, g, :], x3[:, p, g, feature_chunk(k)], ident[:])
                        last.then_inc(s_x3t, 1)
                if a is not None:
                    for h in range(KH):
                        pe.wait_ge(s_rhl, due(a, KH, h + 1))
                    pe.wait_ge(s_sqsum, due(a, 1, 1))
                    for g in range(G):
                        split_product(ps[:, g, 0:D + 2], lambda s, k: rT[s][:, k, g, :], lambda w, k: W2[w][:, k, :], KH)
                        mm(ps[:, g, SQ:SQ + 1], sqsum[:, 0, g, :], mean_row[:, 0:1], start=True, stop=True
                           ).then_inc(s_ym, 1)
                if c is not None:
                    pe.wait_ge(s_x3hi, due(c, KD, KD))
                    pe.wait_ge(s_x3lo, due(c, KD, KD))
                    for g in range(G):
                        last = mm(halves(6 + g // 2)[:, g % 2, :], adjTm[:, p, g, :], x3[:, p, g, :], start=True, stop=True)
                        if g % 2:
                            last.then_inc(s_z, 1)
                    for g in range(G):
                        if g < 2:
                            pe.wait_ge(s_zcp, due(c, 2, g + 1))
                        else:
                            pe.wait_ge(s_uz, due(c, G, g - 1))
                            pe.wait_ge(s_v, due(c, G, g - 1))
                        split_product(ps[:, 6 + g % 2, :], lambda s, k: x3T[s][:, k, g, :], lambda w, k: WUV[w][:, k, :], KD
                                      ).then_inc(s_uv, 1)
                if a is not None:
                    pe.wait_ge(s_y, due(a, G, G))
                    for g in range(G):
                        last = mm(halves(g // 2)[:, g % 2, :], PT[:, g, :], y[:, g, :], start=True, stop=True)
                        if g % 2:
                            last.then_inc(s_py, 1)

            schedule(pe, phase)

        @block.vector
        def _(dve):
            V = nc.vector

            def spread(col, n):
                return col.unsqueeze(2).to_broadcast([N, G, n])

            V.memset(mean_row[:], 1.0 / DH)
            V.memset(neg_half[:], -0.5)
            for k in range(KH):
                V.memset(W2[0][:, k, D:D + 1].bitcast(fp32), 1.0 / DH)
                V.memset(W2[0][:, k, D + 1:D + 2].bitcast(fp32), 0.0)
                V.memset(W2[1][:, k, D:D + 2].bitcast(fp32), 0.0)
            dve.wait_ge(s_const, CONSTS)
            V.tensor_scalar(smask[:], nmask[:], SCALE, None, ALU.mult)
            V.tensor_scalar(no_loop[:], diag[:], 0.0, None, ALU.is_equal)
            for k in range(KH):
                V.tensor_scalar(w2g[:, k, :], raw_w2[:, k, :], gamma_sb[:, k:k + 1], None, ALU.mult)
            dve.drain()
            V.tensor_copy(W1[0][:], raw_w1).then_inc(s_w2g, 1)
            V.tensor_copy(WGAT[0][:], raw_gat)
            V.tensor_copy(WGCN[0][:], raw_gcn)
            dve.drain()
            V.tensor_tensor(W1[1][:], raw_w1, W1[0][:].bitcast(fp32), ALU.subtract)
            V.tensor_tensor(WGAT[1][:], raw_gat, WGAT[0][:].bitcast(fp32), ALU.subtract)
            V.tensor_tensor(WGCN[1][:], raw_gcn, WGCN[0][:].bitcast(fp32), ALU.subtract)
            dve.wait_ge(s_prep_mm, 1)
            V.tensor_copy(beta_w2[:], ps[:, 1, 0:D])
            V.tensor_copy(wa_row[:], halves(2))
            for k in range(KD):
                V.tensor_copy(raw_uv[:, k, 0:D], ps[:, 3 + k, 0:D])
            for k in range(KH):
                V.tensor_tensor(w2g[:, k, :], w2g[:, k, :], ps[:, 0, 0:D], ALU.subtract)
            dve.drain()
            V.tensor_copy(W2[0][:, :, 0:D], w2g)
            V.tensor_copy(WUV[0][:], raw_uv)
            dve.drain()
            V.tensor_tensor(W2[1][:, :, 0:D], w2g, W2[0][:, :, 0:D].bitcast(fp32), ALU.subtract)
            V.tensor_tensor(WUV[1][:], raw_uv, WUV[0][:].bitcast(fp32), ALU.subtract)
            dve.drain()
            V.memset(Be[:], 0.0).then_inc(s_prep, 1)

            def norm_statistics(layer, v):
                for g in range(G):
                    V.bn_stats(bn6[:, layer, g, :], v[:, g, :])
                dve.drain()
                for g in range(G):
                    V.bn_aggr(mv[:, layer, g, :], bn6[:, layer, g, :])
                dve.drain()
                V.tensor_scalar(vare[:, layer, :], mv[:, layer, :, 1], EPS, None, ALU.add)
                V.tensor_scalar(nmean[:, layer, :], mv[:, layer, :, 0], -1.0, None, ALU.mult)
                dve.drain()
                V.engine_nop().then_inc(s_lnst[layer], 1)

            def low_part(lo, hi, full):
                return V.tensor_tensor(lo, full, hi.bitcast(fp32), ALU.subtract)

            def phase(p, a, b, c, t):
                if a is not None:
                    dve.wait_ge(s_loaded[p], 24 * (a - p) + 48)
                    for g in range(G):
                        V.tensor_scalar(H[:, g, :], adj_sb[:, p, g, :], 0.0, None, ALU.not_equal, ALU.add,
                                        accum_out=rowsum[:, g:g + 1])
                    dve.drain()
                    for g in range(G):
                        V.tensor_tensor_reduce(out=HD[:, g, :], in0=H[:, g, :], in1=wrow[:, p, g, :], scale=1.0,
                                               scalar=0.0, op0=ALU.mult, op1=ALU.add, accum_out=Dn[:, g:g + 1])
                    before(dve, s_ATd, a, 1)
                    V.tensor_tensor(deg[:], rowsum[:], no_loop[:, bass.ds(a * G, G)], ALU.add)
                    dve.drain()
                    V.scalar_tensor_tensor(Dpos[:], Dn[:], 0.0, Dn[:], ALU.is_gt, ALU.mult)
                    dve.drain()
                    V.scalar_tensor_tensor(Dsafe[:], Dn[:], 0.0, Dpos[:], ALU.is_le, ALU.add)
                    dve.drain()
                    V.reciprocal(Drec[:], Dsafe[:])
                    dve.drain()
                    V.scalar_tensor_tensor(Dinv[:], Dn[:], 0.0, Drec[:], ALU.is_gt, ALU.mult)
                    dve.drain()
                    V.tensor_tensor(HD[:], H[:], spread(Dinv[:], N), ALU.mult).then_inc(s_HD, 1)
                if b is not None:
                    dve.drain()
                    dve.wait_ge(s_x1, due(b, 1, 1))
                    for g in range(G):
                        for half in range(2):
                            V.tensor_tensor_reduce(out=waste[:, half, :], in0=x1[:, 1 - p, g, :], in1=wa_row[:, half, :],
                                                   scale=1.0, scalar=0.0, op0=ALU.mult, op1=ALU.add,
                                                   accum_out=wh[:, half, g:g + 1])
                        dve.drain()
                    V.engine_nop().then_inc(s_wh, 1)
                if c is not None:
                    for k in range(KD):
                        dve.wait_ge(s_nxhi, due(c, KD, k + 1))
                        low_part(nxT[1][:, k, :, :], nxT[0][:, k, :, :], graphs(6 + k)).then_inc(s_nxlo, 1)
                if a is not None:
                    dve.wait_ge(s_adjTcp, due(a, 1, 1))
                    for g in range(G):
                        V.tensor_scalar(HT[:, g, :], adjT[:, g, :], 0.0, None, ALU.not_equal, ALU.add,
                                        accum_out=Be[:, g:g + 1])
                    V.tensor_scalar(negb[:, p, :, :], adjT[:], 0.5, NEG_INF, ALU.is_le, ALU.mult)
                    dve.drain()
                    V.tensor_scalar(Bemax[:], Be[:], 1.0, None, ALU.max)
                    dve.drain()
                    V.reciprocal(Binv[:], Bemax[:]).then_inc(s_HT, 1)
                    V.tensor_tensor(AT[:], HT[:], ident[:].unsqueeze(1).to_broadcast([N, G, N]), ALU.max
                                    ).then_inc(s_AT, 1)
                if c is not None:
                    for half in range(2):
                        dve.wait_ge(s_agg, due(c, 2, half + 1))
                        for g in (2 * half, 2 * half + 1):
                            last = V.scalar_tensor_tensor(v2[:, g, :], halves(6 + half)[:, g % 2, :],
                                                          dinv[:, p, g:g + 1], gcnb_row[:], ALU.mult, ALU.add)
                        last.then_inc(s_aggb, 1)
                if t is not None:
                    dve.wait_ge(s_wrow, due(t, 1, 1))
                    V.reduce_max(wmax[:], ps[0:G, 5, 0:N], AX.X)
                    dve.drain()
                    V.tensor_scalar(nwmax[:], wmax[:], -1.0, None, ALU.mult).then_inc(s_wmax, 1)
                if c is not None:
                    for half in range(2):
                        dve.wait_ge(s_th, due(c, 2, half + 1))
                        gs = slice(2 * half, 2 * half + 2)
                        V.tensor_tensor(v2[:, gs, :], v2[:, gs, :], x2[:, p, gs, :], ALU.add)
                    dve.drain()
                    norm_statistics(2, v2)
                if b is not None:
                    dve.wait_ge(s_zb, due(b, 1, 1))
                    V.tensor_tensor(score[:], score[:], negb[:, 1 - p, :, :], ALU.add)
                    dve.drain()
                    V.scalar_tensor_tensor(score[:], score[:], SLOPE, score[:], ALU.mult, ALU.max)
                    dve.drain()
                    V.tensor_reduce(emax[:], score[:], AX.X, ALU.max)
                    dve.drain()
                    V.tensor_scalar(nemax[:], emax[:], -1.0, None, ALU.mult).then_inc(s_el, 1)
                if t is not None:
                    dve.wait_ge(s_pexp, due(t, 1, 1))
                    V.reciprocal(prec[:], psum_[:])
                    dve.drain()
                    V.tensor_scalar(prow[:], pexp[:], prec[:], None, ALU.mult).then_inc(s_prow, 1)
                if a is not None:
                    for k in range(KD):
                        dve.wait_ge(s_pxhi, due(a, KD, k + 1))
                        low_part(pxT[1][:, k, :, :], pxT[0][:, k, :, :], graphs((3 + k) % 4)).then_inc(s_pxlo, 1)
                if b is not None:
                    dve.wait_ge(s_eexp, due(b, 1, 1))
                    V.reciprocal(erec[:], esum[:])
                    dve.drain()
                    V.tensor_tensor(score[:], score[:], spread(erec[:], N), ALU.mult).then_inc(s_att, 1)
                if t is not None:
                    dve.wait_ge(s_pps, due(t, 1, 1))
                    V.tensor_copy(pcol[:], ps[:, 5, N:N + G]).then_inc(s_pcol, 1)
                    dve.drain()
                    for g in range(G):
                        V.scalar_tensor_tensor(v3[:, g, :], vals[:, g, :], pcol[:, g:g + 1], x3[:, 1 - p, g, :],
                                               ALU.mult, ALU.add)
                    dve.drain()
                    norm_statistics(3, v3)
                if a is not None:
                    for h in range(KH):
                        dve.wait_ge(s_r, due(a, KH, h + 1))
                        V.tensor_copy(rT[0][:, h, :, :], r[:, h, :, :])
                        dve.drain()
                        low_part(rT[1][:, h, :, :], rT[0][:, h, :, :], r[:, h, :, :]).then_inc(s_rhl, 1)
                    V.scalar_tensor_tensor(v0[:], x_sb[:, p, :, :], 2.0,
                                           b2_row[:].unsqueeze(1).to_broadcast([N, G, D]), ALU.mult, ALU.add
                                           ).then_inc(s_xb, 1)
                if b is not None:
                    for k in range(KD):
                        dve.wait_ge(s_axhi, due(b, KD, k + 1))
                        low_part(axT[1][:, k, :, :], axT[0][:, k, :, :], graphs(5 - k)).then_inc(s_axlo, 1)
                if c is not None:
                    for k in range(KD):
                        dve.wait_ge(s_x3hi, due(c, KD, k + 1))
                        low_part(x3T[1][:, k, :, :], x3T[0][:, k, :, :], graphs(6 + k)).then_inc(s_x3lo, 1)
                if b is not None:
                    for half in range(2):
                        gs = slice(2 * half, 2 * half + 2)
                        dve.wait_ge(s_hexp, due(b, 2, half + 1))
                        V.scalar_tensor_tensor(v1[:, gs, :], halves(4 + half), 0.0, x1[:, 1 - p, gs, :],
                                               ALU.max, ALU.add).then_inc(s_hres, 1)
                        dve.drain()
                        V.scalar_tensor_tensor(v1[:, gs, :], hexp[:, gs, :], 1.0, v1[:, gs, :], ALU.min, ALU.add)
                    dve.drain()
                    norm_statistics(1, v1)
                if a is not None:
                    dve.wait_ge(s_ym, due(a, G, G))
                    V.tensor_copy(hmean[:], ps[:, 0:G, D])
                    dve.drain()
                    V.tensor_tensor(hmean2[:], hmean[:], hmean[:], ALU.mult)
                    dve.drain()
                    V.tensor_tensor(hvar[:], ps[:, 0:G, SQ], hmean2[:], ALU.subtract)
                    dve.drain()
                    V.tensor_scalar(hvare[:], hvar[:], 0.0, EPS, ALU.max, ALU.add).then_inc(s_hvar, 1)
                if c is not None:
                    for g in range(G):
                        dve.wait_ge(s_v, due(c, G, g + 1))
                        dve.wait_ge(s_zcp, due(c, 2, g // 2 + 1))
                        V.tensor_tensor_reduce(out=waste[:, g % 2, :], in0=ps[:, 6 + g % 2, 0:D], in1=z[:, g, :],
                                               scale=1.0, scalar=0.0, op0=ALU.mult, op1=ALU.add,
                                               accum_out=wraw[:, g:g + 1]).then_inc(s_uz, 1)
                        dve.drain()
                    V.tensor_tensor(wcol[:], wraw[:], smask[:, bass.ds(c * G, G)], ALU.mult).then_inc(s_wcol, 1)
                if a is not None:
                    dve.wait_ge(s_hrstd, due(a, 1, 1))
                    for g in range(G):
                        V.scalar_tensor_tensor(y[:, g, :], ps[:, g, 0:D], hrstd[:, g:g + 1], beta_w2[:],
                                               ALU.mult, ALU.add).then_inc(s_y, 1)
                    for half in range(2):
                        gs = slice(2 * half, 2 * half + 2)
                        dve.wait_ge(s_py, due(a, 2, half + 1))
                        V.tensor_tensor(v0[:, gs, :], halves(half), v0[:, gs, :], ALU.add).then_inc(s_v0, 1)
                    dve.drain()
                    norm_statistics(0, v0)

            schedule(dve, phase)

        @block.scalar
        def _(act):
            A = nc.scalar.activation

            def norm_apply(layer, dst, v, done):
                for g in range(G):
                    last = A(dst[:, g, :], v[:, g, :], ACT.Identity, scale=rstd[:, layer, g:g + 1],
                             bias=nmr[:, layer, g:g + 1])
                last.then_inc(done, 1)

            act.wait_ge(s_prep, 1)

            def phase(p, a, b, c, t):
                if c is not None:
                    for k in range(KD):
                        act.wait_ge(s_nx, due(c, KD, k + 1))
                        A(nxT[0][:, k, :, :], graphs(6 + k), ACT.Copy).then_inc(s_nxhi, 1)
                if a is not None:
                    act.wait_ge(s_adjT, due(a, 1, 1))
                    before(act, s_ATd, a, 1)
                    A(adjT[:], graphs(0), ACT.Copy).then_inc(s_adjTcp, 1)
                    act.wait_ge(s_HDTps, due(a, 1, 1))
                    A(HDT[:], graphs(1), ACT.Copy).then_inc(s_HDT, 1)
                if c is not None:
                    for half in range(2):
                        gs = slice(2 * half, 2 * half + 2)
                        act.wait_ge(s_aggb, due(c, 2, half + 1))
                        A(v2[:, gs, :], v2[:, gs, :], ACT.Tanh).then_inc(s_th, 1)
                if t is not None:
                    act.wait_ge(s_wmax, due(t, 1, 1))
                    A(pexp[:], ps[0:G, 5, 0:N], ACT.Exp, bias=nwmax[:], accum_out=psum_[:])
                    act.drain()
                    A(pexp[:, 0:1], pexp[:, 0:1], ACT.Copy).then_inc(s_pexp, 1)
                if a is not None:
                    act.wait_ge(s_Gps, due(a, 1, 1))
                    A(PT[:], graphs(2), ACT.Copy).then_inc(s_PT, 1)
                if b is not None:
                    act.wait_ge(s_bc, due(b, 1, 1))
                    for g in range(G):
                        last = A(score[:, g, :], graphs(4)[:, g, :], ACT.Identity, bias=wh[:, 1, g:g + 1])
                    last.then_inc(s_zb, 1)
                if c is not None:
                    act.wait_ge(s_lnrs[2], due(c, 1, 1))
                    norm_apply(2, x3[:, p, :, :], v2, s_x3)
                if b is not None:
                    act.wait_ge(s_el, due(b, 1, 1))
                    for g in range(G):
                        A(score[:, g, :], score[:, g, :], ACT.Exp, bias=nemax[:, g:g + 1], accum_out=esum[:, g:g + 1])
                    act.drain()
                    A(esum[:, 0:1], esum[:, 0:1], ACT.Copy).then_inc(s_eexp, 1)
                if a is not None:
                    for k in range(KD):
                        act.wait_ge(s_px, due(a, KD, k + 1))
                        A(pxT[0][:, k, :, :], graphs((3 + k) % 4), ACT.Copy).then_inc(s_pxhi, 1)
                    for h in range(KH):
                        act.wait_ge(s_h, due(a, KH, h + 1))
                        A(r[:, h, :, :], graphs((1 + h) % 4), ACT.Relu, bias=b1_sb[:, h:h + 1]).then_inc(s_r, 1)
                        act.drain()
                        if h == 0:
                            before(act, s_sqsum, a, 1)
                        A(sq[:, h, :, :], r[:, h, :, :], ACT.Square).then_inc(s_sq, 1)
                if t is not None:
                    act.wait_ge(s_lnrs[3], due(t, 1, 1))
                    before(act, s_stored, t, 16)
                    norm_apply(3, x4, v3, s_x4)
                if b is not None:
                    for k in range(KD):
                        act.wait_ge(s_ax, due(b, KD, k + 1))
                        A(axT[0][:, k, :, :], graphs(5 - k), ACT.Copy).then_inc(s_axhi, 1)
                    for half in range(2):
                        act.wait_ge(s_hp, due(b, 2, half + 1))
                        A(hexp[:, 2 * half:2 * half + 2, :], halves(4 + half), ACT.Exp).then_inc(s_hexp, 1)
                if c is not None:
                    for k in range(KD):
                        act.wait_ge(s_x3t, due(c, KD, k + 1))
                        A(x3T[0][:, k, :, :], graphs(6 + k), ACT.Copy).then_inc(s_x3hi, 1)
                    for half in range(2):
                        act.wait_ge(s_z, due(c, 2, half + 1))
                        A(z[:, 2 * half:2 * half + 2, :], halves(6 + half), ACT.Copy).then_inc(s_zcp, 1)
                if b is not None:
                    act.wait_ge(s_lnrs[1], due(b, 1, 1))
                    norm_apply(1, x2[:, 1 - p, :, :], v1, s_x2)
                if c is not None:
                    for g in range(G):
                        act.wait_ge(s_uv, due(c, G, g + 1))
                        A(vals[:, g, :], ps[:, 6 + g % 2, D:2 * D], ACT.Copy).then_inc(s_v, 1)
                if a is not None:
                    act.wait_ge(s_lnrs[0], due(a, 1, 1))
                    norm_apply(0, x1[:, p, :, :], v0, s_x1)

            schedule(act, phase)

        @block.gpsimd
        def _(pool):
            P = nc.gpsimd
            P.memset(ident[:], 0.0)
            pool.drain()
            P.affine_select(out=ident[:], in_=ident[:], compare_op=ALU.not_equal, fill=1.0, base=0,
                            pattern=[[-1, N]], channel_multiplier=1).then_inc(s_ident, 1)
            pool.wait_ge(s_prep, 1)

            def spread(col, n):
                return col.unsqueeze(2).to_broadcast([N, G, n])

            def norm_scale(layer, g):
                pool.wait_ge(s_lnst[layer], due(g, 1, 1))
                P.tensor_tensor(rstd[:, layer, :], vare[:, layer, :], neg_half[:], ALU.pow)
                pool.drain()
                P.tensor_tensor(nmr[:, layer, :], nmean[:, layer, :], rstd[:, layer, :], ALU.mult
                                ).then_inc(s_lnrs[layer], 1)

            def phase(p, a, b, c, t):
                if a is not None:
                    pool.wait_ge(s_HT, due(a, 1, 1))
                    P.tensor_tensor(HTB[:], HT[:], spread(Binv[:], N), ALU.mult).then_inc(s_HTB, 1)
                if c is not None:
                    norm_scale(2, c)
                if t is not None:
                    norm_scale(3, t)
                if a is not None:
                    pool.wait_ge(s_sq, due(a, KH, 2))
                    P.tensor_tensor(sqsum[:, 0, :, :], sq[:, 0, :, :], sq[:, 1, :, :], ALU.add)
                    pool.wait_ge(s_sq, due(a, KH, 4))
                    P.tensor_tensor(sqsum[:, 1, :, :], sq[:, 2, :, :], sq[:, 3, :, :], ALU.add)
                    pool.drain()
                    P.tensor_tensor(sqsum[:, 0, :, :], sqsum[:, 0, :, :], sqsum[:, 1, :, :], ALU.add).then_inc(s_sqsum, 1)
                if b is not None:
                    norm_scale(1, b)
                if a is not None:
                    pool.wait_ge(s_hvar, due(a, 1, 1))
                    P.tensor_tensor(hrstd[:], hvare[:], neg_half[:], ALU.pow).then_inc(s_hrstd, 1)
                    if c is not None:
                        pool.wait_ge(s_aggb, due(c, 2, 2))
                        pool.wait_ge(s_z, due(c, 2, 2))
                    pool.wait_ge(s_AT, due(a, 1, 1))
                    pool.wait_ge(s_adjTcp, due(a, 1, 1))
                    P.tensor_tensor(dinv[:, p, :], deg[:], neg_half[:], ALU.pow)
                    P.tensor_tensor(adjTm[:, p, :, :], adjT[:], spread(nmask[:, bass.ds(a * G, G)], N), ALU.mult)
                    pool.drain()
                    P.tensor_tensor(ATd[:, p, :, :], AT[:], spread(dinv[:, p, :], N), ALU.mult).then_inc(s_ATd, 1)
                    norm_scale(0, a)

            schedule(pool, phase)


def kernel(**inputs):
    import numpy as np
    import concourse.bacc as bacc
    from concourse.bass_utils import run_bass_kernel_spmd

    def plain(name):
        return np.ascontiguousarray(inputs[name])

    def turned(name):
        return np.ascontiguousarray(np.asarray(inputs[name]).T)

    def columns(name):
        return np.ascontiguousarray(np.asarray(inputs[name]).reshape(-1, 128).T)

    arrays = {
        "x": plain("x"), "adj": plain("adj"), "nodemask_t": turned("nodemask"),
        "w1_t": turned("L0_gnn_W1"), "b1_cols": columns("L0_gnn_b1"), "gamma_cols": columns("L0_gnn_gamma"),
        "beta_cols": columns("L0_gnn_beta"), "w2_t": turned("L0_gnn_W2"), "b2": plain("L0_gnn_b2"),
        "gat_w": plain("L1_gnn_W"), "gat_w_t": turned("L1_gnn_W"), "gat_a_cols": columns("L1_gnn_a"),
        "gcn_w": plain("L2_gnn_W"), "gcn_b": plain("L2_gnn_b"),
        "wqk_t": turned("L3_gnn_Wqk"), "wv": plain("L3_gnn_Wv"),
    }
    nc = bacc.Bacc("TRN2", target_bir_lowering=False, num_devices=1)
    arrays = {f"in_{name}": a for name, a in arrays.items()}
    args = [nc.dram_tensor(name, a.shape, mybir.dt.from_np(a.dtype), kind="ExternalInput").ap()
            for name, a in arrays.items()]
    out = nc.dram_tensor("out_x", inputs["x"].shape, mybir.dt.float32, kind="ExternalOutput").ap()
    gnn_stack_kernel(nc, *args, out)
    return run_bass_kernel_spmd(nc, [arrays], core_ids=[0]).results[0]["out_x"]
```

```python
import concourse.bass as bass
from concourse import mybir
from contextlib import ExitStack


def gnn_stack_kernel(
    nc: bass.Bass,
    x: bass.AP,
    adj: bass.AP,
    nodemask_t: bass.AP,
    w1_t: bass.AP,
    b1_cols: bass.AP,
    gamma_cols: bass.AP,
    beta_cols: bass.AP,
    w2_t: bass.AP,
    b2: bass.AP,
    gat_w: bass.AP,
    gat_w_t: bass.AP,
    gat_a_cols: bass.AP,
    gcn_w: bass.AP,
    gcn_b: bass.AP,
    wqk_t: bass.AP,
    wv: bass.AP,
    out: bass.AP,
):
    fp32 = mybir.dt.float32
    f32r = mybir.dt.float32r
    ALU = mybir.AluOpType
    ACT = mybir.ActivationFunctionType
    AX = mybir.AxisListType

    NGRAPH, N, D = x.shape
    DH = w1_t.shape[1]
    G = 4
    NG = NGRAPH // G
    KD = D // N
    KH = DH // N
    EPS = 1e-5
    NEG_INF = -9000000000000000.0
    SLOPE = 0.2
    SCALE = 1.0 / float(D) ** 0.5
    Y_BANK = (2, 3, 0, 1)
    UV_BANK = (2, 3, 6, 7)
    SQ = D + 4
    CONSTS = 16 * 15

    ctx = ExitStack()
    with ctx:
        def sb(name, shape, dt=fp32):
            return ctx.enter_context(nc.sbuf_tensor(name, shape, dt))

        def sem(name):
            return ctx.enter_context(nc.semaphore(name))

        ident = sb("ident", [N, N])
        mean_row = sb("mean_row", [N, N])
        neg_half = sb("neg_half", [N, G])
        nmask = sb("nmask", [N, NGRAPH])
        smask = sb("smask", [N, NGRAPH])
        no_loop = sb("no_loop", [N, NGRAPH])
        diag = sb("diag", [N, NGRAPH])
        b1_sb = sb("b1_sb", [N, KH])
        gamma_sb = sb("gamma_sb", [N, KH])
        beta_sb = sb("beta_sb", [N, KH])
        b2_row = sb("b2_row", [N, D])
        b2_half = sb("b2_half", [N, D])
        gcnb_row = sb("gcnb_row", [N, D])
        a_sb = sb("a_sb", [N, 2 * KD])
        beta_w2 = sb("beta_w2", [N, D])
        wa_row = sb("wa_row", [N, 2, D])
        W1 = [sb(f"w1_{s}", [N, KD, DH], f32r) for s in ("hi", "lo")]
        W2 = [sb(f"w2_{s}", [N, KH, D + 2], f32r) for s in ("hi", "lo")]
        WGAT = [sb(f"wgat_{s}", [N, KD, D], f32r) for s in ("hi", "lo")]
        WGCN = [sb(f"wgcn_{s}", [N, KD, D], f32r) for s in ("hi", "lo")]
        WUV = [sb(f"wuv_{s}", [N, KD, 2 * D], f32r) for s in ("hi", "lo")]

        adj_sb = sb("adj_sb", [N, 2, G, N])
        x_sb = sb("x_sb", [N, 2, G, D])
        wrow = sb("wrow", [N, 2, G, N])
        H = sb("H", [N, G, N])
        rowsum = sb("rowsum", [N, G])
        deg = sb("deg", [N, G])
        Dn = sb("Dn", [N, G])
        Dpos = sb("Dpos", [N, G])
        Dsafe = sb("Dsafe", [N, G])
        Drec = sb("Drec", [N, G])
        Dinv = sb("Dinv", [N, G])
        HD = sb("HD", [N, G, N])
        HT = sb("HT", [N, G, N])
        Be = sb("Be", [N, G])
        Bemax = sb("Bemax", [N, G])
        Binv = sb("Binv", [N, G])
        HTB = sb("HTB", [N, G, N])
        HDT = sb("HDT", [N, G, N])
        PT = sb("PT", [N, 2, G, N])
        adjT = sb("adjT", [N, G, N])
        AT = sb("AT", [N, G, N])
        pxT = [sb(f"pxT_{s}", [N, KD, G, N], f32r) for s in ("hi", "lo")]
        r = sb("r", [N, KH, G, N])
        rT = [sb(f"rT_{s}", [N, KH, G, N], f32r) for s in ("hi", "lo")]
        sq = r
        sqsum = sb("sqsum", [N, 2, G, N])
        hmean = sb("hmean", [N, G])
        hmean2 = sb("hmean2", [N, G])
        hvar = sb("hvar", [N, G])
        hvare = sb("hvare", [N, G])
        hrstd = sb("hrstd", [N, G])
        y = sb("y", [N, G, D])
        xb = sb("xb", [N, G, D])
        v0 = sb("v0", [N, G, D])
        negb = sb("negb", [N, 2, G, N])
        ATd = sb("ATd", [N, 2, G, N])
        adjTm = sb("adjTm", [N, 2, G, N])
        dinv = sb("dinv", [N, 2, G])

        x1 = sb("x1", [N, 2, G, D])
        wh = sb("wh", [N, 2, G])
        score = sb("score", [N, G, N])
        emax = sb("emax", [N, G])
        nemax = sb("nemax", [N, G])
        esum = sb("esum", [N, G])
        erec = sb("erec", [N, G])
        axT = [sb(f"axT_{s}", [N, KD, G, N], f32r) for s in ("hi", "lo")]
        hexp = sb("hexp", [N, G, D])
        v1 = sb("v1", [N, G, D])

        x2 = sb("x2", [N, 2, G, D])
        nxT = [sb(f"nxT_{s}", [N, KD, G, N], f32r) for s in ("hi", "lo")]
        v2 = sb("v2", [N, G, D])
        x3 = sb("x3", [N, 2, G, D])
        x3T = nxT
        z = sb("z", [N, G, D])
        wraw = sb("wraw", [N, G])
        wcol = sb("wcol", [N, G])
        vals = sb("vals", [N, G, D])

        wmax = sb("wmax", [G, 1])
        nwmax = sb("nwmax", [G, 1])
        pexp = sb("pexp", [G, N])
        psum_ = sb("psum_", [G, 1])
        prec = sb("prec", [G, 1])
        prow = sb("prow", [G, N])
        pcol = sb("pcol", [N, G])
        v3 = sb("v3", [N, G, D])

        waste_sb = sb("waste_sb", [N, 4, D], mybir.dt.bfloat16)

        def waste(n):
            return waste_sb[:, n % 4, :]

        def place(tile, chunks):
            return tile[:].rearrange("p g d -> p (g d)").rearrange("p (k n) -> p k n", k=chunks)

        raw_w1 = place(v3, KD)
        raw_w2 = place(vals, KH)
        w2g = place(v2, KH)
        raw_qk_t = place(z, 2 * KD)
        raw_uv = place(v1, KD)
        raw_gat, raw_gat_t = y[:, 0:2, :], y[:, 2:4, :]
        raw_gcn = hexp[:, 0:2, :]

        bn6 = sb("bn6", [N, 4, G, 6])
        mv = sb("mv", [N, 4, G, 2])
        vare = sb("vare", [N, 4, G])
        nmean = sb("nmean", [N, 4, G])
        rstd = sb("rstd", [N, 4, G])
        nmr = sb("nmr", [N, 4, G])

        ps = ctx.enter_context(nc.psum_tensor("ps", [N, 8, 512], fp32))

        def graphs(bank):
            return ps[:, bank, :].rearrange("p (g n) -> p g n", g=G)

        def halves(bank):
            return ps[:, bank, :].rearrange("p (g d) -> p g d", g=2)

        s_ident = sem("s_ident")
        s_w2g = sem("s_w2g")
        s_const = sem("s_const")
        s_prep_mm = sem("s_prep_mm")
        s_prep = sem("s_prep")
        s_loaded = [sem("s_loaded0"), sem("s_loaded1")]
        s_stored = sem("s_stored")
        s_HD = sem("s_HD")
        s_adjT = sem("s_adjT")
        s_adjTcp = sem("s_adjTcp")
        s_HT = sem("s_HT")
        s_AT = sem("s_AT")
        s_HTB = sem("s_HTB")
        s_HDTps = sem("s_HDTps")
        s_HDT = sem("s_HDT")
        s_Gps = sem("s_Gps")
        s_PT = sem("s_PT")
        s_px = sem("s_px")
        s_pxhi = sem("s_pxhi")
        s_pxlo = sem("s_pxlo")
        s_h = sem("s_h")
        s_r = sem("s_r")
        s_sq = sem("s_sq")
        s_rhi = sem("s_rhi")
        s_rlo = sem("s_rlo")
        s_sqsum = sem("s_sqsum")
        s_ym = sem("s_ym")
        s_hvar = sem("s_hvar")
        s_hrstd = sem("s_hrstd")
        s_y = sem("s_y")
        s_py = sem("s_py")
        s_v0 = sem("s_v0")
        s_xb = sem("s_xb")
        s_lnst = [sem(f"s_lnst{i}") for i in range(4)]
        s_lnrs = [sem(f"s_lnrs{i}") for i in range(4)]
        s_x1 = sem("s_x1")
        s_x2 = sem("s_x2")
        s_x3 = sem("s_x3")
        s_x4 = sem("s_x4")
        s_wh = sem("s_wh")
        s_bc = sem("s_bc")
        s_zb = sem("s_zb")
        s_el = sem("s_el")
        s_eexp = sem("s_eexp")
        s_att = sem("s_att")
        s_ax = sem("s_ax")
        s_axhi = sem("s_axhi")
        s_axlo = sem("s_axlo")
        s_hp = sem("s_hp")
        s_hexp = sem("s_hexp")
        s_hres = sem("s_hres")
        s_nx = sem("s_nx")
        s_nxhi = sem("s_nxhi")
        s_nxlo = sem("s_nxlo")
        s_agg = sem("s_agg")
        s_aggb = sem("s_aggb")
        s_th = sem("s_th")
        s_v2 = sem("s_v2")
        s_x3t = sem("s_x3t")
        s_x3hi = sem("s_x3hi")
        s_x3lo = sem("s_x3lo")
        s_z = sem("s_z")
        s_zcp = sem("s_zcp")
        s_uv = sem("s_uv")
        s_uz = sem("s_uz")
        s_v = sem("s_v")
        s_wcol = sem("s_wcol")
        s_wrow = sem("s_wrow")
        s_wmax = sem("s_wmax")
        s_pexp = sem("s_pexp")
        s_prow = sem("s_prow")
        s_pps = sem("s_pps")
        s_pcol = sem("s_pcol")
        s_ATd = sem("s_ATd")
        s_adjTm = sem("s_adjTm")
        s_pv = sem("s_pv")
        s_v3 = sem("s_v3")

        block = ctx.enter_context(nc.Block())

        def due(g, per, n):
            return g * per + n

        def before(eng, semaphore, g, per):
            if not (isinstance(g, int) and g == FIRST):
                eng.wait_ge(semaphore, g * per)

        FIRST = 0

        def schedule(eng, phase):
            def live(g):
                return g if 0 <= g < NG else None

            def single(n):
                phase(n % 2, live(n + 1), live(n), live(n - 1), live(n - 2), live(n - 3))

            for n in range(-1, 4):
                single(n)
            with eng.Fori(0, (NG - 6) // 2) as j:
                for u in range(2):
                    phase(u, 2 * j + 5 + u, 2 * j + 4 + u, 2 * j + 3 + u, 2 * j + 2 + u, 2 * j + 1 + u)
            for n in range(NG - 2, NG + 3):
                single(n)

        @block.sync
        def _(sp):
            def load(g, q):
                sp.dma_start(adj_sb[:, q, :, :], adj[bass.ds(g * G, G), :, :].rearrange("g c e -> c g e")
                             ).then_inc(s_loaded[q], 16)
                sp.dma_start(wrow[:, q, :, :], adj[bass.ds(g * G, G), 0, :].unsqueeze(0).to_broadcast([N, G, N])
                             ).then_inc(s_loaded[q], 16)
                sp.dma_start(x_sb[:, q, :, :], x[bass.ds(g * G, G), :, :].rearrange("g n d -> n g d")
                             ).then_inc(s_loaded[q], 16)

            def rows(w):
                return w.rearrange("(k p) n -> p k n", p=N)

            load(0, 0)
            sp.dma_start(raw_w2, rows(w2_t)).then_inc(s_const, 16)
            sp.dma_start(diag[:], adj.rearrange("g n m -> g (n m)")[:, 0:N * N:N + 1].rearrange("g n -> n g"),
                         allow_slow_non_contiguous=True).then_inc(s_const, 16)
            sp.dma_start(nmask[:], nodemask_t).then_inc(s_const, 16)
            sp.dma_start(raw_w1, rows(w1_t)).then_inc(s_const, 16)
            sp.dma_start(b1_sb[:], b1_cols).then_inc(s_const, 16)
            sp.dma_start(gamma_sb[:], gamma_cols).then_inc(s_const, 16)
            sp.dma_start(beta_sb[:], beta_cols).then_inc(s_const, 16)
            sp.dma_start(b2_row[:], b2.unsqueeze(0).to_broadcast([N, D])).then_inc(s_const, 16)
            sp.dma_start(a_sb[:], gat_a_cols).then_inc(s_const, 16)
            sp.dma_start(raw_gat, rows(gat_w)).then_inc(s_const, 16)
            sp.dma_start(raw_gat_t, rows(gat_w_t)).then_inc(s_const, 16)
            sp.dma_start(raw_gcn, rows(gcn_w)).then_inc(s_const, 16)
            sp.dma_start(gcnb_row[:], gcn_b.unsqueeze(0).to_broadcast([N, D])).then_inc(s_const, 16)
            sp.dma_start(raw_qk_t, rows(wqk_t)).then_inc(s_const, 16)
            sp.dma_start(raw_uv[:, :, D:2 * D], rows(wv)).then_inc(s_const, 16)
            load(1, 1)

            def phase(p, f, a, b, c, t):
                if a is not None and not (isinstance(a, int) and a + 2 >= NG):
                    sp.wait_ge(s_adjT, due(a, 1, 1))
                    sp.wait_ge(s_HD, due(a, 1, 1))
                    sp.wait_ge(s_px, due(a, KD, KD))
                    sp.wait_ge(s_xb, due(a, 1, 1))
                    load(a + 2, p)
                if t is not None:
                    sp.wait_ge(s_x4, due(t, 1, 1))
                    sp.dma_start(out[bass.ds(t * G, G), :, :].rearrange("g n d -> n g d"), v3[:]
                                 ).then_inc(s_stored, 16)

            schedule(sp, phase)
            sp.wait_ge(s_stored, 16 * NG)

        @block.tensor
        def _(pe):
            mm = nc.tensor.matmul

            pe.wait_ge(s_const, CONSTS)
            pe.wait_ge(s_ident, 1)
            pe.wait_ge(s_w2g, 1)
            for k in range(KH):
                mm(ps[:, 0, 0:D], mean_row[:], w2g[:, k, :], start=k == 0, stop=k == KH - 1)
            for k in range(KH):
                mm(ps[:, 1, 0:D], beta_sb[:, k:k + 1].to_broadcast([N, N]), raw_w2[:, k, :],
                   start=k == 0, stop=k == KH - 1)
            for half in range(2):
                for k in range(KD):
                    mm(ps[:, 2, half * D:(half + 1) * D],
                       a_sb[:, half * KD + k:half * KD + k + 1].to_broadcast([N, N]), raw_gat_t[:, k, :],
                       start=k == 0, stop=k == KD - 1)
            for m in range(KD):
                for k in range(KD):
                    last = mm(ps[:, 3 + m, 0:D], raw_qk_t[:, k, m * N:(m + 1) * N], raw_qk_t[:, KD + k, :],
                              start=k == 0, stop=k == KD - 1)
            last.then_inc(s_prep_mm, 1)
            pe.wait_ge(s_prep, 1)

            def split_product(dst, left, right, chunks):
                for k in range(chunks):
                    for n, (s, w) in enumerate(((0, 0), (0, 1), (1, 0))):
                        last = mm(dst, left(s, k), right(w, k), start=k == 0 and n == 0,
                                  stop=k == chunks - 1 and n == 2)
                return last

            def feature_chunk(k):
                return slice(k * N, (k + 1) * N)

            def phase(p, f, a, b, c, t):
                if c is not None:
                    pe.wait_ge(s_x2, due(c, 1, 1))
                    pe.wait_ge(s_ATd, due(c, 1, 1))
                    before(pe, s_uz, c, G)
                    for k in range(KD):
                        for g in range(G):
                            last = mm(graphs(6 + k)[:, g, :], x2[:, p, g, feature_chunk(k)], ATd[:, p, g, :],
                                      start=True, stop=True)
                        last.then_inc(s_nx, 1)
                if t is not None:
                    pe.wait_ge(s_wcol, due(t, 1, 1))
                    mm(ps[0:G, 5, 0:N], wcol[:], ident[:], start=True, stop=True).then_inc(s_wrow, 1)
                if a is not None:
                    pe.wait_ge(s_PT, due(a, 1, 1))
                    before(pe, s_v0, a, 2)
                    for k in range(KD):
                        for g in range(G):
                            last = mm(graphs(k)[:, g, :], x_sb[:, p, g, feature_chunk(k)], PT[:, p, g, :],
                                      start=True, stop=True)
                        last.then_inc(s_px, 1)
                if c is not None:
                    pe.wait_ge(s_nxhi, due(c, KD, KD))
                    pe.wait_ge(s_nxlo, due(c, KD, KD))
                    for g in range(G):
                        last = split_product(halves(6 + g // 2)[:, g % 2, :],
                                             lambda s, k: nxT[s][:, k, g, :], lambda w, k: WGCN[w][:, k, :], KD)
                        if g % 2:
                            last.then_inc(s_agg, 1)
                if a is not None:
                    pe.wait_ge(s_pxhi, due(a, KD, KD))
                    pe.wait_ge(s_pxlo, due(a, KD, KD))
                    for h in range(KH):
                        split_product(ps[:, (2 + h) % 4, :],
                                      lambda s, k: W1[s][:, k, feature_chunk(h)],
                                      lambda w, k: pxT[w][:, k, :, :].rearrange("p g n -> p (g n)"), KD
                                      ).then_inc(s_h, 1)
                if t is not None:
                    pe.wait_ge(s_prow, due(t, 1, 1))
                    mm(ps[:, 5, N:N + G], prow[:], ident[0:G, 0:G], start=True, stop=True).then_inc(s_pps, 1)
                if b is not None:
                    pe.wait_ge(s_wh, due(b, 1, 1))
                    for g in range(G):
                        last = mm(graphs(4)[:, g, :], wh[:, 0, g:g + 1].to_broadcast([N, N]), ident[:],
                                  start=True, stop=True)
                    last.then_inc(s_bc, 1)
                if a is not None:
                    for g in range(G):
                        for k in range(KH):
                            if g == 0:
                                pe.wait_ge(s_rlo, due(a, KH, k + 1))
                            for n, (s, w) in enumerate(((0, 0), (0, 1), (1, 0))):
                                mm(ps[:, Y_BANK[g], 0:D + 2], rT[s][:, k, g, :], W2[w][:, k, :],
                                   start=k == 0 and n == 0, stop=k == KH - 1 and n == 2)
                    pe.wait_ge(s_sqsum, due(a, 1, 1))
                    for g in range(G):
                        last = mm(ps[:, Y_BANK[g], SQ:SQ + 1], sqsum[:, 0, g, :], mean_row[:, 0:1], start=True, stop=True)
                    last.then_inc(s_ym, 1)
                if b is not None:
                    pe.wait_ge(s_att, due(b, 1, 1))
                    if t is not None:
                        pe.wait_ge(s_pcol, due(t, 1, 1))
                    for k in range(KD):
                        for g in range(G):
                            last = mm(graphs(5 - k)[:, g, :], x1[:, 1 - p, g, feature_chunk(k)], score[:, g, :],
                                      start=True, stop=True)
                        last.then_inc(s_ax, 1)
                if c is not None:
                    pe.wait_ge(s_x3, due(c, 1, 1))
                    for k in range(KD):
                        for g in range(G):
                            last = nc.tensor.transpose(graphs(6 + k)[:, g, :], x3[:, p, g, feature_chunk(k)], ident[:])
                        last.then_inc(s_x3t, 1)
                if b is not None:
                    pe.wait_ge(s_axhi, due(b, KD, KD))
                    pe.wait_ge(s_axlo, due(b, KD, KD))
                    for g in range(G):
                        last = split_product(halves(4 + g // 2)[:, g % 2, :],
                                             lambda s, k: axT[s][:, k, g, :], lambda w, k: WGAT[w][:, k, :], KD)
                        if g % 2:
                            last.then_inc(s_hp, 1)
                if c is not None:
                    pe.wait_ge(s_x3hi, due(c, KD, KD))
                    pe.wait_ge(s_x3lo, due(c, KD, KD))
                    pe.wait_ge(s_adjTm, due(c, 1, 1))
                    for g in range(G):
                        last = mm(halves(6 + g // 2)[:, g % 2, :], adjTm[:, p, g, :], x3[:, p, g, :], start=True, stop=True)
                        if g % 2:
                            last.then_inc(s_z, 1)
                if f is not None:
                    pe.wait_ge(s_loaded[1 - p], 24 * (f - (1 - p)) + 48)
                    if b is not None:
                        pe.wait_ge(s_hres, due(b, 2, 2))
                    for g in range(G):
                        last = nc.tensor.transpose(graphs(4)[:, g, :], adj_sb[:, 1 - p, g, :], ident[:])
                    last.then_inc(s_adjT, 1)
                    pe.wait_ge(s_HD, due(f, 1, 1))
                    for g in range(G):
                        last = nc.tensor.transpose(graphs(5)[:, g, :], HD[:, g, :], ident[:])
                    last.then_inc(s_HDTps, 1)
                if a is not None:
                    pe.wait_ge(s_y, due(a, G, G))
                    for g in range(G):
                        last = mm(halves(g // 2)[:, g % 2, :], PT[:, p, g, :], y[:, g, :], start=True, stop=True)
                        if g % 2:
                            last.then_inc(s_py, 1)
                if c is not None:
                    for g in range(G):
                        if g == 0 and a is not None:
                            pe.wait_ge(s_y, due(a, G, G))
                        if g == 2:
                            pe.wait_ge(s_zcp, due(c, 2, 2))
                        split_product(ps[:, UV_BANK[g], :], lambda s, k: x3T[s][:, k, g, :], lambda w, k: WUV[w][:, k, :], KD
                                      ).then_inc(s_uv, 1)
                if f is not None:
                    pe.wait_ge(s_HTB, due(f, 1, 1))
                    pe.wait_ge(s_HDT, due(f, 1, 1))
                    for g in range(G):
                        last = mm(graphs(4)[:, g, :], HTB[:, g, :], HDT[:, g, :], start=True, stop=True)
                    last.then_inc(s_Gps, 1)

            schedule(pe, phase)

        @block.vector
        def _(dve):
            V = nc.vector

            def spread(col, n):
                return col.unsqueeze(2).to_broadcast([N, G, n])

            V.memset(mean_row[:], 1.0 / DH)
            V.memset(neg_half[:], -0.5)
            for k in range(KH):
                V.memset(W2[0][:, k, D:D + 1].bitcast(fp32), 1.0 / DH)
                V.memset(W2[0][:, k, D + 1:D + 2].bitcast(fp32), 0.0)
                V.memset(W2[1][:, k, D:D + 2].bitcast(fp32), 0.0)
            dve.wait_ge(s_const, CONSTS)
            V.tensor_scalar(smask[:], nmask[:], SCALE, None, ALU.mult)
            V.tensor_scalar(b2_half[:], b2_row[:], 0.5, None, ALU.mult)
            V.tensor_scalar(no_loop[:], diag[:], 0.0, None, ALU.is_equal)
            for k in range(KH):
                V.tensor_scalar(w2g[:, k, :], raw_w2[:, k, :], gamma_sb[:, k:k + 1], None, ALU.mult)
            dve.drain()
            V.tensor_copy(W1[0][:], raw_w1).then_inc(s_w2g, 1)
            V.tensor_copy(WGAT[0][:], raw_gat)
            V.tensor_copy(WGCN[0][:], raw_gcn)
            dve.drain()
            V.tensor_tensor(W1[1][:], raw_w1, W1[0][:].bitcast(fp32), ALU.subtract)
            V.tensor_tensor(WGAT[1][:], raw_gat, WGAT[0][:].bitcast(fp32), ALU.subtract)
            V.tensor_tensor(WGCN[1][:], raw_gcn, WGCN[0][:].bitcast(fp32), ALU.subtract)
            dve.wait_ge(s_prep_mm, 1)
            V.tensor_copy(beta_w2[:], ps[:, 1, 0:D])
            V.tensor_copy(wa_row[:], halves(2))
            for k in range(KD):
                V.tensor_copy(raw_uv[:, k, 0:D], ps[:, 3 + k, 0:D])
            for k in range(KH):
                V.tensor_tensor(w2g[:, k, :], w2g[:, k, :], ps[:, 0, 0:D], ALU.subtract)
            dve.drain()
            V.tensor_copy(W2[0][:, :, 0:D], w2g)
            V.tensor_copy(WUV[0][:], raw_uv)
            dve.drain()
            V.tensor_tensor(W2[1][:, :, 0:D], w2g, W2[0][:, :, 0:D].bitcast(fp32), ALU.subtract)
            V.tensor_tensor(WUV[1][:], raw_uv, WUV[0][:].bitcast(fp32), ALU.subtract)
            dve.drain()
            V.memset(Be[:], 0.0).then_inc(s_prep, 1)

            def norm_statistics(layer, v):
                for g in range(G):
                    V.bn_stats(bn6[:, layer, g, :], v[:, g, :])
                dve.drain()
                for g in range(G):
                    V.bn_aggr(mv[:, layer, g, :], bn6[:, layer, g, :])
                dve.drain()
                V.tensor_scalar(vare[:, layer, :], mv[:, layer, :, 1], EPS, None, ALU.add)
                V.tensor_scalar(nmean[:, layer, :], mv[:, layer, :, 0], -1.0, None, ALU.mult).then_inc(s_lnst[layer], 1)

            def low_part(lo, hi, full):
                return V.tensor_tensor(lo, full, hi.bitcast(fp32), ALU.subtract)

            def phase(p, f, a, b, c, t):
                if c is not None:
                    for k in range(KD):
                        dve.wait_ge(s_nxhi, due(c, KD, k + 1))
                        low_part(nxT[1][:, k, :, :], nxT[0][:, k, :, :], graphs(6 + k)).then_inc(s_nxlo, 1)
                if t is not None:
                    dve.wait_ge(s_wrow, due(t, 1, 1))
                    V.reduce_max(wmax[:], ps[0:G, 5, 0:N], AX.X)
                    dve.drain()
                    V.tensor_scalar(nwmax[:], wmax[:], -1.0, None, ALU.mult).then_inc(s_wmax, 1)
                if a is not None:
                    for k in range(KD):
                        dve.wait_ge(s_pxhi, due(a, KD, k + 1))
                        low_part(pxT[1][:, k, :, :], pxT[0][:, k, :, :], graphs(k)).then_inc(s_pxlo, 1)
                if t is not None:
                    dve.wait_ge(s_pexp, due(t, 1, 1))
                    V.reciprocal(prec[:], psum_[:])
                    dve.drain()
                    V.tensor_scalar(prow[:], pexp[:], prec[:], None, ALU.mult).then_inc(s_prow, 1)
                if c is not None:
                    for half in range(2):
                        dve.wait_ge(s_agg, due(c, 2, half + 1))
                        for g in (2 * half, 2 * half + 1):
                            last = V.scalar_tensor_tensor(v2[:, g, :], halves(6 + half)[:, g % 2, :],
                                                          dinv[:, p, g:g + 1], gcnb_row[:], ALU.mult, ALU.add)
                        last.then_inc(s_aggb, 1)
                if b is not None:
                    dve.drain()
                    dve.wait_ge(s_x1, due(b, 1, 1))
                    for g in range(G):
                        if g == 2:
                            dve.drain()
                        for half in range(2):
                            last = V.tensor_tensor_reduce(out=waste(2 * g + half), in0=x1[:, 1 - p, g, :],
                                                          in1=wa_row[:, half, :], scale=1.0, scalar=0.0,
                                                          op0=ALU.mult, op1=ALU.add, accum_out=wh[:, half, g:g + 1])
                    last.then_inc(s_wh, 1)
                if c is not None:
                    dve.wait_ge(s_v2, due(c, 1, 1))
                    norm_statistics(2, v2)
                if a is not None:
                    for h in range(KH):
                        dve.wait_ge(s_rhi, due(a, KH, h + 1))
                        low_part(rT[1][:, h, :, :], rT[0][:, h, :, :], r[:, h, :, :]).then_inc(s_rlo, 1)
                if b is not None:
                    dve.wait_ge(s_zb, due(b, 1, 1))
                    V.tensor_tensor(score[:], score[:], negb[:, 1 - p, :, :], ALU.add)
                    dve.drain()
                    V.scalar_tensor_tensor(score[:], score[:], SLOPE, score[:], ALU.mult, ALU.max)
                    dve.drain()
                    V.tensor_reduce(emax[:], score[:], AX.X, ALU.max)
                    dve.drain()
                    V.tensor_scalar(nemax[:], emax[:], -1.0, None, ALU.mult).then_inc(s_el, 1)
                if f is not None:
                    dve.wait_ge(s_loaded[1 - p], 24 * (f - (1 - p)) + 48)
                    before(dve, s_ATd, f, 1)
                    for g in range(G):
                        V.tensor_scalar(H[:, g, :], adj_sb[:, 1 - p, g, :], 0.0, None, ALU.not_equal, ALU.add,
                                        accum_out=rowsum[:, g:g + 1])
                    dve.drain()
                    for g in range(G):
                        V.tensor_tensor_reduce(out=HD[:, g, :], in0=H[:, g, :], in1=wrow[:, 1 - p, g, :], scale=1.0,
                                               scalar=0.0, op0=ALU.mult, op1=ALU.add, accum_out=Dn[:, g:g + 1])
                    V.tensor_tensor(deg[:], rowsum[:], no_loop[:, bass.ds(f * G, G)], ALU.add)
                    dve.drain()
                if b is not None:
                    dve.wait_ge(s_eexp, due(b, 1, 1))
                    V.reciprocal(erec[:], esum[:])
                    dve.drain()
                    V.tensor_tensor(score[:], score[:], spread(erec[:], N), ALU.mult).then_inc(s_att, 1)
                if f is not None:
                    V.scalar_tensor_tensor(Dpos[:], Dn[:], 0.0, Dn[:], ALU.is_gt, ALU.mult)
                    dve.drain()
                    V.scalar_tensor_tensor(Dsafe[:], Dn[:], 0.0, Dpos[:], ALU.is_le, ALU.add)
                    dve.drain()
                    V.reciprocal(Drec[:], Dsafe[:])
                    dve.drain()
                    V.scalar_tensor_tensor(Dinv[:], Dn[:], 0.0, Drec[:], ALU.is_gt, ALU.mult)
                    dve.drain()
                    V.tensor_tensor(HD[:], H[:], spread(Dinv[:], N), ALU.mult).then_inc(s_HD, 1)
                if t is not None:
                    dve.wait_ge(s_v3, due(t, 1, 1))
                    norm_statistics(3, v3)
                if b is not None:
                    for k in range(KD):
                        dve.wait_ge(s_axhi, due(b, KD, k + 1))
                        low_part(axT[1][:, k, :, :], axT[0][:, k, :, :], graphs(5 - k)).then_inc(s_axlo, 1)
                if a is not None:
                    dve.wait_ge(s_ym, due(a, 1, 1))
                    V.tensor_copy(hmean[:], ps[:, 0:G, D])
                    dve.drain()
                    V.tensor_tensor(hmean2[:], hmean[:], hmean[:], ALU.mult)
                    dve.drain()
                    V.tensor_tensor(hvar[:], ps[:, 0:G, SQ], hmean2[:], ALU.subtract)
                    dve.drain()
                    V.tensor_scalar(hvare[:], hvar[:], 0.0, EPS, ALU.max, ALU.add).then_inc(s_hvar, 1)
                if c is not None:
                    for k in range(KD):
                        dve.wait_ge(s_x3hi, due(c, KD, k + 1))
                        low_part(x3T[1][:, k, :, :], x3T[0][:, k, :, :], graphs(6 + k)).then_inc(s_x3lo, 1)
                if a is not None:
                    dve.wait_ge(s_hrstd, due(a, 1, 1))
                    for g in range(G):
                        V.scalar_tensor_tensor(y[:, g, :], ps[:, Y_BANK[g], 0:D],
                                               hrstd[:, Y_BANK[g]:Y_BANK[g] + 1], beta_w2[:],
                                               ALU.mult, ALU.add).then_inc(s_y, 1)
                if b is not None:
                    for half in range(2):
                        gs = slice(2 * half, 2 * half + 2)
                        dve.wait_ge(s_hexp, due(b, 2, half + 1))
                        V.scalar_tensor_tensor(v1[:, gs, :], halves(4 + half), 0.0, x1[:, 1 - p, gs, :],
                                               ALU.max, ALU.add).then_inc(s_hres, 1)
                    dve.drain()
                    V.scalar_tensor_tensor(v1[:], hexp[:], 1.0, v1[:], ALU.min, ALU.add)
                    dve.drain()
                    norm_statistics(1, v1)
                if f is not None:
                    dve.wait_ge(s_adjTcp, due(f, 1, 1))
                    for g in range(G):
                        V.tensor_scalar(HT[:, g, :], adjT[:, g, :], 0.0, None, ALU.not_equal, ALU.add,
                                        accum_out=Be[:, g:g + 1])
                    dve.drain()
                    V.tensor_scalar(Bemax[:], Be[:], 1.0, None, ALU.max)
                    dve.drain()
                    V.reciprocal(Binv[:], Bemax[:]).then_inc(s_HT, 1)
                    V.tensor_scalar(negb[:, 1 - p, :, :], adjT[:], 0.5, NEG_INF, ALU.is_le, ALU.mult)
                    V.tensor_tensor(AT[:], HT[:], ident[:].unsqueeze(1).to_broadcast([N, G, N]), ALU.max
                                    ).then_inc(s_AT, 1)
                if a is not None:
                    for half in range(2):
                        gs = slice(2 * half, 2 * half + 2)
                        dve.wait_ge(s_py, due(a, 2, half + 1))
                        V.scalar_tensor_tensor(v0[:, gs, :], xb[:, gs, :], 2.0, halves(half), ALU.mult, ALU.add
                                               ).then_inc(s_v0, 1)
                    dve.drain()
                    norm_statistics(0, v0)
                if c is not None:
                    for g in range(G):
                        dve.wait_ge(s_v, due(c, G, g + 1))
                        V.tensor_tensor_reduce(out=waste(g), in0=ps[:, UV_BANK[g], 0:D], in1=z[:, g, :],
                                               scale=1.0, scalar=0.0, op0=ALU.mult, op1=ALU.add,
                                               accum_out=wraw[:, g:g + 1]).then_inc(s_uz, 1)
                    dve.drain()
                    V.tensor_tensor(wcol[:], wraw[:], smask[:, bass.ds(c * G, G)], ALU.mult).then_inc(s_wcol, 1)

            schedule(dve, phase)

        @block.scalar
        def _(act):
            A = nc.scalar.activation

            def norm_apply(layer, dst, v, done):
                for g in range(G):
                    last = A(dst[:, g, :], v[:, g, :], ACT.Identity, scale=rstd[:, layer, g:g + 1],
                             bias=nmr[:, layer, g:g + 1])
                last.then_inc(done, 1)

            act.wait_ge(s_prep, 1)

            def phase(p, f, a, b, c, t):
                if c is not None:
                    for k in range(KD):
                        act.wait_ge(s_nx, due(c, KD, k + 1))
                        A(nxT[0][:, k, :, :], graphs(6 + k), ACT.Copy).then_inc(s_nxhi, 1)
                if a is not None:
                    for k in range(KD):
                        act.wait_ge(s_px, due(a, KD, k + 1))
                        A(pxT[0][:, k, :, :], graphs(k), ACT.Copy).then_inc(s_pxhi, 1)
                if t is not None:
                    act.wait_ge(s_wmax, due(t, 1, 1))
                    A(pexp[:], ps[0:G, 5, 0:N], ACT.Exp, bias=nwmax[:], accum_out=psum_[:]).then_inc(s_pexp, 1)
                if c is not None:
                    for half in range(2):
                        gs = slice(2 * half, 2 * half + 2)
                        act.wait_ge(s_aggb, due(c, 2, half + 1))
                        A(v2[:, gs, :], v2[:, gs, :], ACT.Tanh).then_inc(s_th, 1)
                if a is not None:
                    before(act, s_sqsum, a, 1)
                    for h in range(KH):
                        act.wait_ge(s_h, due(a, KH, h + 1))
                        A(r[:, h, :, :], graphs((2 + h) % 4), ACT.Relu, bias=b1_sb[:, h:h + 1]).then_inc(s_r, 1)
                        A(rT[0][:, h, :, :], graphs((2 + h) % 4), ACT.Relu, bias=b1_sb[:, h:h + 1]).then_inc(s_rhi, 1)
                if t is not None:
                    act.wait_ge(s_pps, due(t, 1, 1))
                    A(pcol[:], ps[:, 5, N:N + G], ACT.Copy).then_inc(s_pcol, 1)
                    act.drain()
                if b is not None:
                    act.wait_ge(s_bc, due(b, 1, 1))
                    for g in range(G):
                        last = A(score[:, g, :], graphs(4)[:, g, :], ACT.Identity, bias=wh[:, 1, g:g + 1])
                    last.then_inc(s_zb, 1)
                if a is not None:
                    for h in range(KH):
                        act.wait_ge(s_rlo, due(a, KH, h + 1))
                        A(sq[:, h, :, :], r[:, h, :, :], ACT.Square).then_inc(s_sq, 1)
                if t is not None:
                    before(act, s_stored, t, 16)
                    for g in range(G):
                        last = A(v3[:, g, :], vals[:, g, :], ACT.Copy, scale=pcol[:, g:g + 1])
                    last.then_inc(s_pv, 1)
                if b is not None:
                    act.wait_ge(s_el, due(b, 1, 1))
                    for g in range(G):
                        last = A(score[:, g, :], score[:, g, :], ACT.Exp, bias=nemax[:, g:g + 1],
                                 accum_out=esum[:, g:g + 1])
                    last.then_inc(s_eexp, 1)
                if c is not None:
                    act.wait_ge(s_lnrs[2], due(c, 1, 1))
                    norm_apply(2, x3[:, p, :, :], v2, s_x3)
                if b is not None:
                    for k in range(KD):
                        act.wait_ge(s_ax, due(b, KD, k + 1))
                        A(axT[0][:, k, :, :], graphs(5 - k), ACT.Copy).then_inc(s_axhi, 1)
                if c is not None:
                    for k in range(KD):
                        act.wait_ge(s_x3t, due(c, KD, k + 1))
                        A(x3T[0][:, k, :, :], graphs(6 + k), ACT.Copy).then_inc(s_x3hi, 1)
                if t is not None:
                    act.wait_ge(s_lnrs[3], due(t, 1, 1))
                    norm_apply(3, v3, v3, s_x4)
                if b is not None:
                    for half in range(2):
                        act.wait_ge(s_hp, due(b, 2, half + 1))
                        A(hexp[:, 2 * half:2 * half + 2, :], halves(4 + half), ACT.Exp).then_inc(s_hexp, 1)
                if f is not None:
                    act.wait_ge(s_adjT, due(f, 1, 1))
                    before(act, s_adjTm, f, 1)
                    A(adjT[:], graphs(4), ACT.Copy).then_inc(s_adjTcp, 1)
                if c is not None:
                    for half in range(2):
                        act.wait_ge(s_z, due(c, 2, half + 1))
                        A(z[:, 2 * half:2 * half + 2, :], halves(6 + half), ACT.Copy).then_inc(s_zcp, 1)
                if b is not None:
                    act.wait_ge(s_lnrs[1], due(b, 1, 1))
                    norm_apply(1, x2[:, 1 - p, :, :], v1, s_x2)
                if c is not None:
                    for g in range(G):
                        act.wait_ge(s_uv, due(c, G, g + 1))
                        A(vals[:, g, :], ps[:, UV_BANK[g], D:2 * D], ACT.Copy).then_inc(s_v, 1)
                if f is not None:
                    act.wait_ge(s_HDTps, due(f, 1, 1))
                    A(HDT[:], graphs(5), ACT.Copy).then_inc(s_HDT, 1)
                    act.wait_ge(s_Gps, due(f, 1, 1))
                    A(PT[:, 1 - p, :, :], graphs(4), ACT.Copy).then_inc(s_PT, 1)
                if a is not None:
                    act.wait_ge(s_lnrs[0], due(a, 1, 1))
                    norm_apply(0, x1[:, p, :, :], v0, s_x1)

            schedule(act, phase)

        @block.gpsimd
        def _(pool):
            P = nc.gpsimd
            P.memset(ident[:], 0.0)
            pool.drain()
            P.affine_select(out=ident[:], in_=ident[:], compare_op=ALU.not_equal, fill=1.0, base=0,
                            pattern=[[-1, N]], channel_multiplier=1).then_inc(s_ident, 1)
            pool.wait_ge(s_prep, 1)

            def spread(col, n):
                return col.unsqueeze(2).to_broadcast([N, G, n])

            def norm_scale(layer, g):
                pool.wait_ge(s_lnst[layer], due(g, 1, 1))
                P.tensor_tensor(rstd[:, layer, :], vare[:, layer, :], neg_half[:], ALU.pow)
                pool.drain()
                P.tensor_tensor(nmr[:, layer, :], nmean[:, layer, :], rstd[:, layer, :], ALU.mult
                                ).then_inc(s_lnrs[layer], 1)

            def phase(p, f, a, b, c, t):
                if a is not None:
                    before(pool, s_v0, a, 2)
                    for g in range(G):
                        last = P.tensor_tensor(xb[:, g, :], x_sb[:, p, g, :], b2_half[:], ALU.add)
                    last.then_inc(s_xb, 1)
                if c is not None:
                    for half in range(2):
                        gs = slice(2 * half, 2 * half + 2)
                        pool.wait_ge(s_th, due(c, 2, half + 1))
                        last = P.tensor_tensor(v2[:, gs, :], v2[:, gs, :], x2[:, p, gs, :], ALU.add)
                    last.then_inc(s_v2, 1)
                    norm_scale(2, c)
                if a is not None:
                    if c is not None:
                        pool.wait_ge(s_aggb, due(c, 2, 2))
                    pool.wait_ge(s_AT, due(a, 1, 1))
                    P.tensor_tensor(dinv[:, p, :], deg[:], neg_half[:], ALU.pow)
                    pool.drain()
                    P.tensor_tensor(ATd[:, p, :, :], AT[:], spread(dinv[:, p, :], N), ALU.mult).then_inc(s_ATd, 1)
                    pool.wait_ge(s_sq, due(a, KH, 2))
                    P.tensor_tensor(sqsum[:, 0, :, :], sq[:, 0, :, :], sq[:, 1, :, :], ALU.add)
                    pool.wait_ge(s_sq, due(a, KH, 4))
                    P.tensor_tensor(sqsum[:, 1, :, :], sq[:, 2, :, :], sq[:, 3, :, :], ALU.add)
                    pool.drain()
                    P.tensor_tensor(sqsum[:, 0, :, :], sqsum[:, 0, :, :], sqsum[:, 1, :, :], ALU.add).then_inc(s_sqsum, 1)
                if t is not None:
                    pool.wait_ge(s_pv, due(t, 1, 1))
                    P.tensor_tensor(v3[:], v3[:], x3[:, 1 - p, :, :], ALU.add).then_inc(s_v3, 1)
                    norm_scale(3, t)
                if a is not None:
                    pool.wait_ge(s_hvar, due(a, 1, 1))
                    P.tensor_tensor(hrstd[:], hvare[:], neg_half[:], ALU.pow).then_inc(s_hrstd, 1)
                    if c is not None:
                        pool.wait_ge(s_z, due(c, 2, 2))
                    P.tensor_tensor(adjTm[:, p, :, :], adjT[:], spread(nmask[:, bass.ds(a * G, G)], N), ALU.mult
                                    ).then_inc(s_adjTm, 1)
                if b is not None:
                    norm_scale(1, b)
                if f is not None:
                    pool.wait_ge(s_HT, due(f, 1, 1))
                    P.tensor_tensor(HTB[:], HT[:], spread(Binv[:], N), ALU.mult).then_inc(s_HTB, 1)
                if a is not None:
                    norm_scale(0, a)

            schedule(pool, phase)


def kernel(**inputs):
    import numpy as np
    import concourse.bacc as bacc
    from concourse.bass_utils import run_bass_kernel_spmd

    def plain(name):
        return np.ascontiguousarray(inputs[name])

    def turned(name):
        return np.ascontiguousarray(np.asarray(inputs[name]).T)

    def columns(name):
        return np.ascontiguousarray(np.asarray(inputs[name]).reshape(-1, 128).T)

    arrays = {
        "x": plain("x"), "adj": plain("adj"), "nodemask_t": turned("nodemask"),
        "w1_t": turned("L0_gnn_W1"), "b1_cols": columns("L0_gnn_b1"), "gamma_cols": columns("L0_gnn_gamma"),
        "beta_cols": columns("L0_gnn_beta"), "w2_t": turned("L0_gnn_W2"), "b2": plain("L0_gnn_b2"),
        "gat_w": plain("L1_gnn_W"), "gat_w_t": turned("L1_gnn_W"), "gat_a_cols": columns("L1_gnn_a"),
        "gcn_w": plain("L2_gnn_W"), "gcn_b": plain("L2_gnn_b"),
        "wqk_t": turned("L3_gnn_Wqk"), "wv": plain("L3_gnn_Wv"),
    }
    nc = bacc.Bacc("TRN2", target_bir_lowering=False, num_devices=1)
    arrays = {f"in_{name}": a for name, a in arrays.items()}
    args = [nc.dram_tensor(name, a.shape, mybir.dt.from_np(a.dtype), kind="ExternalInput").ap()
            for name, a in arrays.items()]
    out = nc.dram_tensor("out_x", inputs["x"].shape, mybir.dt.float32, kind="ExternalOutput").ap()
    gnn_stack_kernel(nc, *args, out)
    return run_bass_kernel_spmd(nc, [arrays], core_ids=[0]).results[0]["out_x"]
```

```python
import concourse.bass as bass
from concourse import mybir
from contextlib import ExitStack


def gnn_stack_kernel(
    nc: bass.Bass,
    x: bass.AP,
    adj: bass.AP,
    nodemask_t: bass.AP,
    w1_t: bass.AP,
    b1_cols: bass.AP,
    gamma_cols: bass.AP,
    beta_cols: bass.AP,
    w2_t: bass.AP,
    b2: bass.AP,
    gat_w: bass.AP,
    gat_w_t: bass.AP,
    gat_a_cols: bass.AP,
    gcn_w: bass.AP,
    gcn_b: bass.AP,
    wqk_t: bass.AP,
    wv: bass.AP,
    out: bass.AP,
):
    fp32 = mybir.dt.float32
    f32r = mybir.dt.float32r
    ALU = mybir.AluOpType
    ACT = mybir.ActivationFunctionType
    AX = mybir.AxisListType

    NGRAPH, N, D = x.shape
    DH = w1_t.shape[1]
    G = 4
    NG = NGRAPH // G
    KD = D // N
    KH = DH // N
    EPS = 1e-5
    TINY = 1.1754944e-38
    NEG_INF = -9000000000000000.0
    FAR = 3.0e38
    SLOPE = 0.2
    SCALE = 1.0 / float(D) ** 0.5
    Y_BANK = (2, 3, 0, 1)
    UV_BANK = (6, 7, 2, 3)
    SHORT = (3,)
    SQ = D + 4
    REST = 16 * 7

    ctx = ExitStack()
    with ctx:
        def sb(name, shape, dt=fp32):
            return ctx.enter_context(nc.sbuf_tensor(name, shape, dt))

        def sem(name):
            return ctx.enter_context(nc.semaphore(name))

        ident = sb("ident", [N, N])
        mean_row = sb("mean_row", [N, N])
        neg_half = sb("neg_half", [N, G])
        eps = sb("eps", [N, G])
        nmask = sb("nmask", [N, NGRAPH])
        smask = sb("smask", [N, NGRAPH])
        no_loop = sb("no_loop", [N, NGRAPH])
        diag = sb("diag", [N, NGRAPH])
        b1_sb = sb("b1_sb", [N, KH])
        gamma_sb = sb("gamma_sb", [N, KH])
        beta_sb = sb("beta_sb", [N, KH])
        b2_row = sb("b2_row", [N, D])
        b2_half = sb("b2_half", [N, D])
        gcnb_row = sb("gcnb_row", [N, D])
        a_sb = sb("a_sb", [N, 2 * KD])
        beta_w2 = sb("beta_w2", [N, D])
        wa_row = sb("wa_row", [N, 2, D])
        W1 = [sb(f"w1_{s}", [N, KD, DH], f32r) for s in ("hi", "lo")]
        W2 = [sb(f"w2_{s}", [N, KH, D + 2], f32r) for s in ("hi", "lo")]
        WGAT = [sb(f"wgat_{s}", [N, KD, D], f32r) for s in ("hi", "lo")]
        WGCN = [sb(f"wgcn_{s}", [N, KD, D], f32r) for s in ("hi", "lo")]
        WUV = [sb(f"wuv_{s}", [N, KD, 2 * D], f32r) for s in ("hi", "lo")]

        adj_sb = sb("adj_sb", [N, 2, G, N])
        x_sb = sb("x_sb", [N, 2, G, D])
        wrow = sb("wrow", [N, 2, G, N])
        H = sb("H", [N, G, N])
        rowsum = sb("rowsum", [N, 2, G])
        deg = sb("deg", [N, G])
        Dn = sb("Dn", [N, G])
        Dsafe = sb("Dsafe", [N, G])
        Drec = sb("Drec", [N, G])
        Dinv = sb("Dinv", [N, G])
        HT = sb("HT", [N, G, N])
        Be = sb("Be", [N, G])
        Bemax = sb("Bemax", [N, G])
        Binv = sb("Binv", [N, G])
        HTB = sb("HTB", [N, G, N])
        HDT = sb("HDT", [N, G, N])
        PT = sb("PT", [N, 2, G, N])
        adjT = sb("adjT", [N, 2, G, N])
        AT = sb("AT", [N, G, N])
        pxT = [sb(f"pxT_{s}", [N, KD, G, N], f32r) for s in ("hi", "lo")]
        r = sb("r", [N, KH, G, N])
        rT = [sb(f"rT_{s}", [N, KH, G, N], f32r) for s in ("hi", "lo")]
        sq = r
        sqsum = sb("sqsum", [N, 2, G, N])
        hmean = sb("hmean", [N, G])
        hmean2 = sb("hmean2", [N, G])
        hvar = sb("hvar", [N, G])
        hvare = sb("hvare", [N, G])
        hrstd = sb("hrstd", [N, G])
        y = sb("y", [N, G, D])
        xb = sb("xb", [N, G, D])
        v0 = sb("v0", [N, G, D])
        negb = sb("negb", [N, 2, G, N])
        ATd = sb("ATd", [N, 2, G, N])
        adjTm = sb("adjTm", [N, 2, G, N])
        dinv = sb("dinv", [N, 2, G])

        x1 = sb("x1", [N, 2, G, D])
        wh = sb("wh", [N, 2, G])
        score = sb("score", [N, G, N])
        nemax = sb("nemax", [N, G])
        esum = sb("esum", [N, G])
        erec = sb("erec", [N, G])
        axT = [sb(f"axT_{s}", [N, KD, G, N], f32r) for s in ("hi", "lo")]
        hexp = sb("hexp", [N, G, D])
        v1 = sb("v1", [N, G, D])

        x2 = sb("x2", [N, 2, G, D])
        nxT = [sb(f"nxT_{s}", [N, KD, G, N], f32r) for s in ("hi", "lo")]
        v2 = sb("v2", [N, G, D])
        x3 = sb("x3", [N, 2, G, D])
        x3T = nxT
        z = sb("z", [N, G, D])
        wraw = sb("wraw", [N, G])
        wcol = sb("wcol", [N, G])
        vals = sb("vals", [N, G, D])

        nwmax = sb("nwmax", [G, 1])
        pexp = sb("pexp", [G, N])
        pexpsum = sb("pexpsum", [G, 1])
        prec = sb("prec", [G, 1])
        prow = sb("prow", [G, N])
        pcol = sb("pcol", [N, G])
        v3 = sb("v3", [N, G, D])

        waste_sb = sb("waste_sb", [N, 4, D], mybir.dt.bfloat16)

        def waste(n):
            return waste_sb[:, n % 4, :]

        def place(tile, chunks):
            return tile[:].rearrange("p g d -> p (g d)").rearrange("p (k n) -> p k n", k=chunks)

        raw_w1 = place(v3, KD)
        raw_w2 = place(vals, KH)
        w2g = place(v2, KH)
        raw_qk_t = place(z, 2 * KD)
        raw_uv = place(v1, KD)
        raw_gat, raw_gat_t = x3[:, 0, 0:2, :], x3[:, 0, 2:4, :]
        raw_gcn = hexp[:, 0:2, :]

        bn6 = sb("bn6", [N, 4, G, 6])
        mv = sb("mv", [N, 4, G, 2])
        vare = sb("vare", [N, 4, G])
        nmean = sb("nmean", [N, 4, G])
        rstd = sb("rstd", [N, 4, G])
        nmr = sb("nmr", [N, 4, G])

        ps = ctx.enter_context(nc.psum_tensor("ps", [N, 8, 512], fp32))

        def graphs(bank):
            return ps[:, bank, :].rearrange("p (g n) -> p g n", g=G)

        def halves(bank):
            return ps[:, bank, :].rearrange("p (g d) -> p g d", g=2)

        s_ident = sem("s_ident")
        s_w2in = sem("s_w2in")
        s_w1in = sem("s_w1in")
        s_nodes = sem("s_nodes")
        s_rest = sem("s_rest")
        s_w2g = sem("s_w2g")
        s_w2mm = sem("s_w2mm")
        s_w2c = sem("s_w2c")
        s_w1hi = sem("s_w1hi")
        s_w2hi = sem("s_w2hi")
        s_w1 = sem("s_w1")
        s_w2 = sem("s_w2")
        s_restmm = sem("s_restmm")
        s_uvcp = sem("s_uvcp")
        s_wahi = sem("s_wahi")
        s_uvhi = sem("s_uvhi")
        s_wa = sem("s_wa")
        s_wuv = sem("s_wuv")
        s_loaded = [sem("s_loaded0"), sem("s_loaded1")]
        s_stored = sem("s_stored")
        s_HD = sem("s_HD")
        s_adjT = sem("s_adjT")
        s_adjTcp = sem("s_adjTcp")
        s_HT = sem("s_HT")
        s_AT = sem("s_AT")
        s_Dinv = sem("s_Dinv")
        s_HTB = sem("s_HTB")
        s_HDTps = sem("s_HDTps")
        s_HDT = sem("s_HDT")
        s_Gps = sem("s_Gps")
        s_PT = sem("s_PT")
        s_px = sem("s_px")
        s_pxhi = sem("s_pxhi")
        s_pxlo = sem("s_pxlo")
        s_h = sem("s_h")
        s_sq = sem("s_sq")
        s_rhi = sem("s_rhi")
        s_rlo = sem("s_rlo")
        s_sqsum = sem("s_sqsum")
        s_ym = sem("s_ym")
        s_hvar = sem("s_hvar")
        s_hrstd = sem("s_hrstd")
        s_y = sem("s_y")
        s_py = sem("s_py")
        s_v0 = sem("s_v0")
        s_xb = sem("s_xb")
        s_lnst = [sem(f"s_lnst{i}") for i in range(4)]
        s_lnrs = [sem(f"s_lnrs{i}") for i in range(4)]
        s_x1 = sem("s_x1")
        s_x2 = sem("s_x2")
        s_x3 = sem("s_x3")
        s_x4 = sem("s_x4")
        s_wh = sem("s_wh")
        s_bc = sem("s_bc")
        s_zb = sem("s_zb")
        s_el = sem("s_el")
        s_eexp = sem("s_eexp")
        s_att = sem("s_att")
        s_ax = sem("s_ax")
        s_axhi = sem("s_axhi")
        s_axlo = sem("s_axlo")
        s_hp = sem("s_hp")
        s_hexp = sem("s_hexp")
        s_hres = sem("s_hres")
        s_nx = sem("s_nx")
        s_nxhi = sem("s_nxhi")
        s_nxlo = sem("s_nxlo")
        s_agg = sem("s_agg")
        s_aggb = sem("s_aggb")
        s_th = sem("s_th")
        s_v2 = sem("s_v2")
        s_x3t = sem("s_x3t")
        s_x3hi = sem("s_x3hi")
        s_x3lo = sem("s_x3lo")
        s_z = sem("s_z")
        s_zcp = sem("s_zcp")
        s_uv = sem("s_uv")
        s_uz = sem("s_uz")
        s_v = sem("s_v")
        s_wcol = sem("s_wcol")
        s_wrow = sem("s_wrow")
        s_wmax = sem("s_wmax")
        s_pexp = sem("s_pexp")
        s_prow = sem("s_prow")
        s_pps = sem("s_pps")
        s_pcol = sem("s_pcol")
        s_ATd = sem("s_ATd")
        s_adjTm = sem("s_adjTm")
        s_pv = sem("s_pv")
        s_v3 = sem("s_v3")

        block = ctx.enter_context(nc.Block())

        def due(g, per, n):
            return g * per + n

        def first(g):
            return isinstance(g, int) and g == 0

        def before(eng, semaphore, g, per):
            if not first(g):
                eng.wait_ge(semaphore, g * per)

        def schedule(eng, phase, middle=None, rest=None):
            def live(g):
                return g if 0 <= g < NG else None

            def single(n):
                phase(n % 2, live(n + 1), live(n), live(n - 1), live(n - 2), live(n - 3))

            single(-1)
            if middle is not None:
                middle()
            single(0)
            if rest is not None:
                rest()
            for n in range(1, 4):
                single(n)
            with eng.Fori(0, (NG - 6) // 2) as j:
                for u in range(2):
                    phase(u, 2 * j + 5 + u, 2 * j + 4 + u, 2 * j + 3 + u, 2 * j + 2 + u, 2 * j + 1 + u)
            for n in range(NG - 2, NG + 3):
                single(n)

        @block.sync
        def _(sp):
            def load(g, q, with_x=True):
                sp.dma_start(adj_sb[:, q, :, :], adj[bass.ds(g * G, G), :, :].rearrange("g c e -> c g e")
                             ).then_inc(s_loaded[q], 16)
                sp.dma_start(wrow[:, q, :, :], adj[bass.ds(g * G, G), 0, :].unsqueeze(0).to_broadcast([N, G, N])
                             ).then_inc(s_loaded[q], 16)
                if with_x:
                    load_x(g, q)

            def load_x(g, q):
                sp.dma_start(x_sb[:, q, :, :], x[bass.ds(g * G, G), :, :].rearrange("g n d -> n g d")
                             ).then_inc(s_loaded[q], 16)

            def rows(w):
                return w.rearrange("(k p) n -> p k n", p=N)

            sp.dma_start(raw_w2, rows(w2_t)).then_inc(s_w2in, 16)
            sp.dma_start(gamma_sb[:], gamma_cols).then_inc(s_w2in, 16)
            sp.dma_start(beta_sb[:], beta_cols).then_inc(s_w2in, 16)
            load(0, 0, with_x=False)
            sp.dma_start(raw_w1, rows(w1_t)).then_inc(s_w1in, 16)
            load_x(0, 0)
            sp.dma_start(b1_sb[:], b1_cols).then_inc(s_w1in, 16)
            sp.dma_start(b2_row[:], b2.unsqueeze(0).to_broadcast([N, D])).then_inc(s_w1in, 16)
            sp.dma_start(diag[:], adj.rearrange("g n m -> g (n m)")[:, 0:N * N:N + 1].rearrange("g n -> n g"),
                         allow_slow_non_contiguous=True).then_inc(s_nodes, 16)
            sp.dma_start(nmask[:], nodemask_t).then_inc(s_nodes, 16)
            load(1, 1)
            sp.dma_start(a_sb[:], gat_a_cols).then_inc(s_rest, 16)
            sp.dma_start(raw_gat_t, rows(gat_w_t)).then_inc(s_rest, 16)
            sp.dma_start(raw_qk_t, rows(wqk_t)).then_inc(s_rest, 16)
            sp.dma_start(raw_gat, rows(gat_w)).then_inc(s_rest, 16)
            sp.dma_start(raw_gcn, rows(gcn_w)).then_inc(s_rest, 16)
            sp.dma_start(raw_uv[:, :, D:2 * D], rows(wv)).then_inc(s_rest, 16)
            sp.dma_start(gcnb_row[:], gcn_b.unsqueeze(0).to_broadcast([N, D])).then_inc(s_rest, 16)

            def phase(p, f, a, b, c, t):
                if a is not None and not (isinstance(a, int) and a + 2 >= NG):
                    sp.wait_ge(s_adjT, due(a, 1, 1))
                    sp.wait_ge(s_HD, due(a, 1, 1))
                    sp.wait_ge(s_px, due(a, KD, KD))
                    sp.wait_ge(s_xb, due(a, 1, 1))
                    load(a + 2, p)
                if t is not None:
                    sp.wait_ge(s_x4, due(t, 2, 2))
                    sp.dma_start(out[bass.ds(t * G, G), :, :].rearrange("g n d -> n g d"), v3[:]
                                 ).then_inc(s_stored, 16)

            schedule(sp, phase)
            sp.wait_ge(s_stored, 16 * NG)

        @block.tensor
        def _(pe):
            mm = nc.tensor.matmul

            pe.wait_ge(s_w2in, 16 * 3)
            pe.wait_ge(s_w2g, 1)
            for k in range(KH):
                mm(ps[:, 6, 0:D], mean_row[:], w2g[:, k, :], start=k == 0, stop=k == KH - 1)
            for k in range(KH):
                last = mm(ps[:, 7, 0:D], beta_sb[:, k:k + 1].to_broadcast([N, N]), raw_w2[:, k, :],
                          start=k == 0, stop=k == KH - 1)
            last.then_inc(s_w2mm, 1)
            pe.wait_ge(s_ident, 1)

            def rest():
                pe.wait_ge(s_rest, REST)
                for half in range(2):
                    for k in range(KD):
                        mm(ps[:, 6, half * D:(half + 1) * D],
                           a_sb[:, half * KD + k:half * KD + k + 1].to_broadcast([N, N]), raw_gat_t[:, k, :],
                           start=k == 0, stop=k == KD - 1)
                for m in range(KD):
                    for k in range(KD):
                        last = mm(ps[:, 7, m * D:(m + 1) * D], raw_qk_t[:, k, m * N:(m + 1) * N],
                                  raw_qk_t[:, KD + k, :], start=k == 0, stop=k == KD - 1)
                last.then_inc(s_restmm, 1)
                pe.wait_ge(s_wa, 1)
                pe.wait_ge(s_wuv, 1)
                pe.wait_ge(s_wa, 2)

            def split_product(dst, left, right, chunks):
                for k in range(chunks):
                    for n, (s, w) in enumerate(((0, 0), (0, 1), (1, 0))):
                        last = mm(dst, left(s, k), right(w, k), start=k == 0 and n == 0,
                                  stop=k == chunks - 1 and n == 2)
                return last

            def feature_chunk(k):
                return slice(k * N, (k + 1) * N)

            def middle():
                pe.wait_ge(s_w1, 1)
                pe.wait_ge(s_w2, 1)

            def phase(p, f, a, b, c, t):
                if a is not None:
                    pe.wait_ge(s_PT, due(a, 1, 1))
                    before(pe, s_v0, a, 2)
                    for k in range(KD):
                        for g in range(G):
                            last = mm(graphs(k)[:, g, :], x_sb[:, p, g, feature_chunk(k)], PT[:, p, g, :],
                                      start=True, stop=True)
                        last.then_inc(s_px, 1)
                if c is not None:
                    pe.wait_ge(s_ATd, due(c, 1, 1))
                    if not first(c):
                        pe.wait_ge(s_uz, due(c - 1, G, 2))
                    for half in range(2):
                        pe.wait_ge(s_x2, due(c, 2, half + 1))
                        for k in range(KD):
                            for g in (2 * half, 2 * half + 1):
                                last = mm(graphs(6 + k)[:, g, :], x2[:, p, g, feature_chunk(k)], ATd[:, p, g, :],
                                          start=True, stop=True)
                            if half:
                                last.then_inc(s_nx, 1)
                if t is not None:
                    pe.wait_ge(s_wcol, due(t, 1, 1))
                    if not (isinstance(t, int) and t == NG - 1):
                        pe.wait_ge(s_hres, due(t + 1, 2, 2))
                    mm(ps[0:G, 5, 0:N], wcol[:], ident[:], start=True, stop=True).then_inc(s_wrow, 1)
                if f is not None:
                    pe.wait_ge(s_loaded[1 - p], 24 * (f - (1 - p)) + 48)
                    before(pe, s_PT, f, 1)
                    if b is not None:
                        before(pe, s_hres, b, 2)
                    for g in range(G):
                        last = nc.tensor.transpose(graphs(4)[:, g, :], adj_sb[:, 1 - p, g, :], ident[:])
                    last.then_inc(s_adjT, 1)
                if c is not None:
                    pe.wait_ge(s_nxlo, due(c, KD, KD))
                    for g in range(G):
                        last = split_product(halves(6 + g // 2)[:, g % 2, :],
                                             lambda s, k: nxT[s][:, k, g, :], lambda w, k: WGCN[w][:, k, :], KD)
                        if g % 2:
                            last.then_inc(s_agg, 1)
                if t is not None:
                    pe.wait_ge(s_prow, due(t, 1, 1))
                    mm(ps[:, 5, N:N + G], prow[:], ident[0:G, 0:G], start=True, stop=True).then_inc(s_pps, 1)
                if f is not None:
                    pe.wait_ge(s_HD, due(f, 1, 1))
                    if t is not None:
                        pe.wait_ge(s_pcol, due(t, 1, 1))
                    for g in range(G):
                        last = nc.tensor.transpose(graphs(5)[:, g, :], H[:, g, :], ident[:])
                    last.then_inc(s_HDTps, 1)
                if a is not None:
                    pe.wait_ge(s_pxlo, due(a, KD, KD))
                    if c is not None:
                        before(pe, s_uz, c, G)
                    for h in range(KH):
                        split_product(ps[:, (2 + h) % 4, :],
                                      lambda s, k: W1[s][:, k, feature_chunk(h)],
                                      lambda w, k: pxT[w][:, k, :, :].rearrange("p g n -> p (g n)"), KD
                                      ).then_inc(s_h, 1)
                if f is not None:
                    pe.wait_ge(s_HTB, due(f, 1, 1))
                    pe.wait_ge(s_HDT, due(f, 1, 1))
                    for g in range(G):
                        last = mm(graphs(4)[:, g, :], HTB[:, g, :], HDT[:, g, :], start=True, stop=True)
                    last.then_inc(s_Gps, 1)
                if b is not None:
                    pe.wait_ge(s_wh, due(b, 1, 1))
                    if f is not None:
                        pe.wait_ge(s_PT, due(f, 1, 1))
                    for g in range(G):
                        last = mm(graphs(4)[:, g, :], wh[:, 0, g:g + 1].to_broadcast([N, N]), ident[:],
                                  start=True, stop=True)
                    last.then_inc(s_bc, 1)
                if a is not None:
                    for g in range(G):
                        for k in range(KH):
                            if g == 0:
                                pe.wait_ge(s_rlo, due(a, KH, k + 1))
                            for n, (s, w) in enumerate(((0, 0), (0, 1), (1, 0))):
                                mm(ps[:, Y_BANK[g], 0:D + 2], rT[s][:, k, g, :], W2[w][:, k, :],
                                   start=k == 0 and n == 0, stop=k == KH - 1 and n == 2)
                    pe.wait_ge(s_sqsum, due(a, 1, 1))
                    for g in range(G):
                        last = mm(ps[:, Y_BANK[g], SQ:SQ + 1], sqsum[:, 0, g, :], mean_row[:, 0:1], start=True, stop=True)
                    last.then_inc(s_ym, 1)
                if b is not None:
                    pe.wait_ge(s_att, due(b, 1, 1))
                    if t is not None and f is None:
                        pe.wait_ge(s_pcol, due(t, 1, 1))
                    for k in range(KD):
                        for g in range(G):
                            last = mm(graphs(5 - k)[:, g, :], x1[:, 1 - p, g, feature_chunk(k)], score[:, g, :],
                                      start=True, stop=True)
                        last.then_inc(s_ax, 1)
                if c is not None:
                    for half in range(2):
                        pe.wait_ge(s_x3, due(c, 2, half + 1))
                        for k in range(KD):
                            for g in (2 * half, 2 * half + 1):
                                last = nc.tensor.transpose(graphs(6 + k)[:, g, :], x3[:, p, g, feature_chunk(k)], ident[:])
                            if half:
                                last.then_inc(s_x3t, 1)
                if b is not None:
                    pe.wait_ge(s_axlo, due(b, KD, KD))
                    for g in range(G):
                        last = split_product(halves(4 + g // 2)[:, g % 2, :],
                                             lambda s, k: axT[s][:, k, g, :], lambda w, k: WGAT[w][:, k, :], KD)
                        if g % 2:
                            last.then_inc(s_hp, 1)
                if c is not None:
                    pe.wait_ge(s_x3lo, due(c, KD, KD))
                    pe.wait_ge(s_adjTm, due(c, 1, 1))
                    for g in range(G):
                        last = mm(halves(6 + g // 2)[:, g % 2, :], adjTm[:, p, g, :], x3[:, p, g, :], start=True, stop=True)
                        if g % 2:
                            last.then_inc(s_z, 1)
                if a is not None:
                    pe.wait_ge(s_y, due(a, G, G))
                    for g in range(G):
                        last = mm(halves(g // 2)[:, g % 2, :], PT[:, p, g, :], y[:, g, :], start=True, stop=True)
                        if g % 2:
                            last.then_inc(s_py, 1)
                if c is not None:
                    for g in range(G):
                        if g == 0:
                            pe.wait_ge(s_zcp, due(c, 2, 2))
                        if g == 2 and a is not None:
                            pe.wait_ge(s_y, due(a, G, G))
                        split_product(ps[:, UV_BANK[g], :], lambda s, k: x3T[s][:, k, g, :], lambda w, k: WUV[w][:, k, :], KD
                                      ).then_inc(s_uv, 1)

            schedule(pe, phase, middle, rest)

        @block.vector
        def _(dve):
            V = nc.vector

            def spread(col, n):
                return col.unsqueeze(2).to_broadcast([N, G, n])

            V.memset(mean_row[:], 1.0 / DH)
            V.memset(neg_half[:], -0.5)
            V.memset(eps[:], EPS)
            for k in range(KH):
                V.memset(W2[0][:, k, D:D + 1].bitcast(fp32), 1.0 / DH)
                V.memset(W2[0][:, k, D + 1:D + 2].bitcast(fp32), 0.0)
                V.memset(W2[1][:, k, D:D + 2].bitcast(fp32), 0.0)
            V.memset(Be[:], 0.0)
            dve.wait_ge(s_w2in, 16 * 3)
            for k in range(KH):
                last = V.tensor_scalar(w2g[:, k, :], raw_w2[:, k, :], gamma_sb[:, k:k + 1], None, ALU.mult)
            last.then_inc(s_w2g, 1)

            def middle():
                dve.wait_ge(s_w2mm, 1)
                for k in range(KH):
                    last = V.tensor_tensor(w2g[:, k, :], w2g[:, k, :], ps[:, 6, 0:D], ALU.subtract)
                last.then_inc(s_w2c, 1)
                V.tensor_copy(beta_w2[:], ps[:, 7, 0:D])
                dve.wait_ge(s_w1hi, 1)
                V.tensor_tensor(W1[1][:], raw_w1, W1[0][:].bitcast(fp32), ALU.subtract).then_inc(s_w1, 1)
                dve.wait_ge(s_w2hi, 1)
                V.tensor_tensor(W2[1][:, :, 0:D], w2g, W2[0][:, :, 0:D].bitcast(fp32), ALU.subtract).then_inc(s_w2, 1)

            def rest():
                dve.wait_ge(s_restmm, 1)
                for k in range(KD):
                    last = V.tensor_copy(raw_uv[:, k, 0:D], halves(7)[:, k, :])
                last.then_inc(s_uvcp, 1)
                V.tensor_copy(wa_row[:], halves(6))
                dve.wait_ge(s_nodes, 16 * 2)
                V.tensor_scalar(smask[:], nmask[:], SCALE, None, ALU.mult)
                dve.wait_ge(s_wahi, 1)
                V.tensor_tensor(WGAT[1][:], raw_gat, WGAT[0][:].bitcast(fp32), ALU.subtract).then_inc(s_wa, 1)
                V.tensor_tensor(WGCN[1][:], raw_gcn, WGCN[0][:].bitcast(fp32), ALU.subtract).then_inc(s_wa, 1)
                dve.wait_ge(s_uvhi, 1)
                V.tensor_tensor(WUV[1][:], raw_uv, WUV[0][:].bitcast(fp32), ALU.subtract).then_inc(s_wuv, 1)
                dve.drain()

            def row_statistics(layer, v, gs):
                for g in gs:
                    V.bn_stats(bn6[:, layer, g, :], v[:, g, :])

            def norm_statistics(layer):
                dve.drain()
                for g in range(G):
                    last = V.bn_aggr(mv[:, layer, g, :], bn6[:, layer, g, :])
                if layer in SHORT:
                    last.then_inc(s_lnst[layer], 1)
                    return
                dve.drain()
                V.tensor_scalar(vare[:, layer, :], mv[:, layer, :, 1], EPS, None, ALU.add)
                V.tensor_scalar(nmean[:, layer, :], mv[:, layer, :, 0], -1.0, None, ALU.mult).then_inc(s_lnst[layer], 1)

            def low_part(lo, hi, full):
                return V.tensor_tensor(lo, full, hi.bitcast(fp32), ALU.subtract)

            def phase(p, f, a, b, c, t):
                if f is not None:
                    dve.wait_ge(s_loaded[1 - p], 24 * (f - (1 - p)) + 48)
                    before(dve, s_HDTps, f, 1)
                    for g in range(G):
                        V.tensor_scalar(H[:, g, :], adj_sb[:, 1 - p, g, :], 0.0, None, ALU.not_equal, ALU.add,
                                        accum_out=rowsum[:, 1 - p, g:g + 1])
                    dve.drain()
                    for g in range(G):
                        V.tensor_tensor_reduce(out=waste(g)[:, 0:N], in0=H[:, g, :], in1=wrow[:, 1 - p, g, :], scale=1.0,
                                               scalar=0.0, op0=ALU.mult, op1=ALU.add, accum_out=Dn[:, g:g + 1])
                    dve.drain()
                if c is not None:
                    for k in range(KD):
                        dve.wait_ge(s_nxhi, due(c, KD, k + 1))
                        low_part(nxT[1][:, k, :, :], nxT[0][:, k, :, :], graphs(6 + k)).then_inc(s_nxlo, 1)
                if t is not None:
                    dve.wait_ge(s_wrow, due(t, 1, 1))
                    V.reduce_max(nwmax[:], ps[0:G, 5, 0:N], AX.X, negate=True).then_inc(s_wmax, 1)
                if f is not None:
                    V.tensor_scalar(Dsafe[:], Dn[:], TINY, None, ALU.max)
                    dve.drain()
                    V.reciprocal(Drec[:], Dsafe[:])
                    dve.drain()
                    V.scalar_tensor_tensor(Dinv[:], Dn[:], 0.0, Drec[:], ALU.is_gt, ALU.mult).then_inc(s_Dinv, 1)
                if t is not None:
                    dve.wait_ge(s_pexp, due(t, 1, 1))
                    V.reciprocal(prec[:], pexpsum[:])
                    dve.drain()
                    V.tensor_scalar(prow[:], pexp[:], prec[:], None, ALU.mult).then_inc(s_prow, 1)
                if a is not None:
                    for k in range(KD):
                        dve.wait_ge(s_pxhi, due(a, KD, k + 1))
                        low_part(pxT[1][:, k, :, :], pxT[0][:, k, :, :], graphs(k)).then_inc(s_pxlo, 1)
                if f is not None:
                    dve.wait_ge(s_adjTcp, due(f, 1, 1))
                    for g in range(G):
                        V.tensor_scalar(HT[:, g, :], adjT[:, 1 - p, g, :], 0.0, None, ALU.not_equal, ALU.add,
                                        accum_out=Be[:, g:g + 1])
                    dve.drain()
                    V.tensor_scalar(Bemax[:], Be[:], 1.0, None, ALU.max)
                    dve.drain()
                    V.reciprocal(Binv[:], Bemax[:]).then_inc(s_HT, 1)
                if c is not None:
                    for half in range(2):
                        dve.wait_ge(s_agg, due(c, 2, half + 1))
                        for g in (2 * half, 2 * half + 1):
                            last = V.scalar_tensor_tensor(v2[:, g, :], halves(6 + half)[:, g % 2, :],
                                                          dinv[:, p, g:g + 1], gcnb_row[:], ALU.mult, ALU.add)
                        last.then_inc(s_aggb, 1)
                if b is not None:
                    for g in range(G):
                        if g == 2:
                            dve.drain()
                        if g % 2 == 0:
                            dve.wait_ge(s_x1, due(b, 2, g // 2 + 1))
                        for half in range(2):
                            last = V.tensor_tensor_reduce(out=waste(2 * g + half), in0=x1[:, 1 - p, g, :],
                                                          in1=wa_row[:, half, :], scale=1.0, scalar=0.0,
                                                          op0=ALU.mult, op1=ALU.add, accum_out=wh[:, half, g:g + 1])
                    last.then_inc(s_wh, 1)
                if c is not None:
                    for half in range(2):
                        dve.wait_ge(s_v2, due(c, 2, half + 1))
                        row_statistics(2, v2, (2 * half, 2 * half + 1))
                    norm_statistics(2)
                if a is not None:
                    for h in range(KH):
                        dve.wait_ge(s_rhi, due(a, KH, h + 1))
                        low_part(rT[1][:, h, :, :], rT[0][:, h, :, :], r[:, h, :, :]).then_inc(s_rlo, 1)
                if b is not None:
                    dve.wait_ge(s_zb, due(b, 1, 1))
                    V.scalar_tensor_tensor(score[:], score[:], SLOPE, score[:], ALU.mult, ALU.max)
                    dve.drain()
                    for g in range(G):
                        last = V.tensor_tensor_reduce(out=score[:, g, :], in0=score[:, g, :], in1=negb[:, 1 - p, g, :],
                                                      scale=-1.0, scalar=FAR, op0=ALU.add, op1=ALU.min,
                                                      accum_out=nemax[:, g:g + 1])
                        if g % 2:
                            last.then_inc(s_el, 1)
                    dve.wait_ge(s_eexp, due(b, 1, 1))
                    V.reciprocal(erec[:], esum[:])
                    dve.drain()
                    V.tensor_tensor(score[:], score[:], spread(erec[:], N), ALU.mult).then_inc(s_att, 1)
                if t is not None:
                    dve.wait_ge(s_v3, due(t, 1, 1))
                    row_statistics(3, v3, range(G))
                    norm_statistics(3)
                if a is not None:
                    dve.wait_ge(s_ym, due(a, 1, 1))
                    V.tensor_copy(hmean[:], ps[:, 0:G, D])
                    dve.drain()
                    V.tensor_tensor(hmean2[:], hmean[:], hmean[:], ALU.mult)
                    dve.drain()
                    V.tensor_tensor(hvar[:], ps[:, 0:G, SQ], hmean2[:], ALU.subtract)
                    dve.drain()
                    V.tensor_scalar(hvare[:], hvar[:], 0.0, EPS, ALU.max, ALU.add).then_inc(s_hvar, 1)
                if b is not None:
                    for k in range(KD):
                        dve.wait_ge(s_axhi, due(b, KD, k + 1))
                        low_part(axT[1][:, k, :, :], axT[0][:, k, :, :], graphs(5 - k)).then_inc(s_axlo, 1)
                if c is not None:
                    for k in range(KD):
                        dve.wait_ge(s_x3hi, due(c, KD, k + 1))
                        low_part(x3T[1][:, k, :, :], x3T[0][:, k, :, :], graphs(6 + k)).then_inc(s_x3lo, 1)
                if a is not None:
                    dve.wait_ge(s_hrstd, due(a, 1, 1))
                    for g in range(G):
                        V.scalar_tensor_tensor(y[:, g, :], ps[:, Y_BANK[g], 0:D],
                                               hrstd[:, Y_BANK[g]:Y_BANK[g] + 1], beta_w2[:],
                                               ALU.mult, ALU.add).then_inc(s_y, 1)
                if b is not None:
                    for half in range(2):
                        gs = slice(2 * half, 2 * half + 2)
                        dve.wait_ge(s_hexp, due(b, 2, half + 1))
                        V.scalar_tensor_tensor(v1[:, gs, :], halves(4 + half), 0.0, x1[:, 1 - p, gs, :],
                                               ALU.max, ALU.add).then_inc(s_hres, 1)
                        dve.drain()
                        V.scalar_tensor_tensor(v1[:, gs, :], hexp[:, gs, :], 1.0, v1[:, gs, :], ALU.min, ALU.add)
                        dve.drain()
                        row_statistics(1, v1, (2 * half, 2 * half + 1))
                    norm_statistics(1)
                if a is not None:
                    for half in range(2):
                        gs = slice(2 * half, 2 * half + 2)
                        dve.wait_ge(s_py, due(a, 2, half + 1))
                        V.scalar_tensor_tensor(v0[:, gs, :], xb[:, gs, :], 2.0, halves(half), ALU.mult, ALU.add
                                               ).then_inc(s_v0, 1)
                    dve.drain()
                    row_statistics(0, v0, range(G))
                    norm_statistics(0)
                if f is not None:
                    before(dve, s_ATd, f, 1)
                    V.tensor_scalar(negb[:, 1 - p, :, :], adjT[:, 1 - p, :, :], 0.5, NEG_INF, ALU.is_le, ALU.mult)
                    V.tensor_tensor(AT[:], HT[:], ident[:].unsqueeze(1).to_broadcast([N, G, N]), ALU.max
                                    ).then_inc(s_AT, 1)
                if c is not None:
                    for g in (0, 1):
                        dve.wait_ge(s_v, due(c, G, g + 1))
                        V.tensor_tensor_reduce(out=waste(g), in0=ps[:, UV_BANK[g], 0:D], in1=z[:, g, :],
                                               scale=1.0, scalar=0.0, op0=ALU.mult, op1=ALU.add,
                                               accum_out=wraw[:, g:g + 1]).then_inc(s_uz, 1)
                    for g in (2, 3):
                        dve.wait_ge(s_v, due(c, G, g + 1))
                        V.tensor_tensor_reduce(out=waste(g), in0=ps[:, UV_BANK[g], 0:D], in1=z[:, g, :],
                                               scale=1.0, scalar=0.0, op0=ALU.mult, op1=ALU.add,
                                               accum_out=wraw[:, g:g + 1]).then_inc(s_uz, 1)

            schedule(dve, phase, middle, rest)

        @block.scalar
        def _(act):
            A = nc.scalar.activation

            def norm_apply(layer, dst, v, done):
                for g in range(G):
                    last = A(dst[:, g, :], v[:, g, :], ACT.Identity, scale=rstd[:, layer, g:g + 1],
                             bias=nmr[:, layer, g:g + 1])
                    if g % 2:
                        last.then_inc(done, 1)

            act.wait_ge(s_w1in, 16 * 3)
            A(W1[0][:], raw_w1, ACT.Copy).then_inc(s_w1hi, 1)

            def middle():
                act.wait_ge(s_w2c, 1)
                A(W2[0][:, :, 0:D], w2g, ACT.Copy).then_inc(s_w2hi, 1)

            def rest():
                act.wait_ge(s_rest, REST)
                A(WGAT[0][:], raw_gat, ACT.Copy)
                A(WGCN[0][:], raw_gcn, ACT.Copy).then_inc(s_wahi, 1)
                act.wait_ge(s_uvcp, 1)
                A(WUV[0][:], raw_uv, ACT.Copy).then_inc(s_uvhi, 1)

            def phase(p, f, a, b, c, t):
                if c is not None:
                    for k in range(KD):
                        act.wait_ge(s_nx, due(c, KD, k + 1))
                        A(nxT[0][:, k, :, :], graphs(6 + k), ACT.Copy).then_inc(s_nxhi, 1)
                if a is not None:
                    for k in range(KD):
                        act.wait_ge(s_px, due(a, KD, k + 1))
                        A(pxT[0][:, k, :, :], graphs(k), ACT.Copy).then_inc(s_pxhi, 1)
                if t is not None:
                    act.wait_ge(s_wmax, due(t, 1, 1))
                    A(pexp[:], ps[0:G, 5, 0:N], ACT.Exp, bias=nwmax[:], accum_out=pexpsum[:]).then_inc(s_pexp, 1)
                if f is not None:
                    act.wait_ge(s_adjT, due(f, 1, 1))
                    if not (isinstance(f, int) and f < 2):
                        act.wait_ge(s_adjTm, due(f - 2, 1, 1))
                    A(adjT[:, 1 - p, :, :], graphs(4), ACT.Copy).then_inc(s_adjTcp, 1)
                if t is not None:
                    act.wait_ge(s_pps, due(t, 1, 1))
                    A(pcol[:], ps[:, 5, N:N + G], ACT.Copy).then_inc(s_pcol, 1)
                    act.drain()
                if f is not None:
                    act.wait_ge(s_HDTps, due(f, 1, 1))
                    A(HDT[:], graphs(5), ACT.Copy).then_inc(s_HDT, 1)
                if c is not None:
                    for half in range(2):
                        gs = slice(2 * half, 2 * half + 2)
                        act.wait_ge(s_aggb, due(c, 2, half + 1))
                        A(v2[:, gs, :], v2[:, gs, :], ACT.Tanh).then_inc(s_th, 1)
                if a is not None:
                    before(act, s_sqsum, a, 1)
                    for h in range(KH):
                        act.wait_ge(s_h, due(a, KH, h + 1))
                        A(r[:, h, :, :], graphs((2 + h) % 4), ACT.Relu, bias=b1_sb[:, h:h + 1])
                        A(rT[0][:, h, :, :], graphs((2 + h) % 4), ACT.Relu, bias=b1_sb[:, h:h + 1]).then_inc(s_rhi, 1)
                if f is not None:
                    act.wait_ge(s_Gps, due(f, 1, 1))
                    A(PT[:, 1 - p, :, :], graphs(4), ACT.Copy).then_inc(s_PT, 1)
                if a is not None:
                    for h in range(KH):
                        act.wait_ge(s_rlo, due(a, KH, h + 1))
                        A(sq[:, h, :, :], r[:, h, :, :], ACT.Square).then_inc(s_sq, 1)
                if b is not None:
                    act.wait_ge(s_bc, due(b, 1, 1))
                    for g in range(G):
                        last = A(score[:, g, :], graphs(4)[:, g, :], ACT.Identity, bias=wh[:, 1, g:g + 1])
                    last.then_inc(s_zb, 1)
                if t is not None:
                    before(act, s_stored, t, 16)
                    for g in range(G):
                        last = A(v3[:, g, :], vals[:, g, :], ACT.Copy, scale=pcol[:, g:g + 1])
                    last.then_inc(s_pv, 1)
                if b is not None:
                    for g in range(G):
                        if g % 2 == 0:
                            act.wait_ge(s_el, due(b, 2, g // 2 + 1))
                        last = A(score[:, g, :], score[:, g, :], ACT.Exp, bias=nemax[:, g:g + 1], scale=-1.0,
                                 accum_out=esum[:, g:g + 1])
                    last.then_inc(s_eexp, 1)
                if c is not None:
                    act.wait_ge(s_lnrs[2], due(c, 1, 1))
                    norm_apply(2, x3[:, p, :, :], v2, s_x3)
                if b is not None:
                    for k in range(KD):
                        act.wait_ge(s_ax, due(b, KD, k + 1))
                        A(axT[0][:, k, :, :], graphs(5 - k), ACT.Copy).then_inc(s_axhi, 1)
                if c is not None:
                    for k in range(KD):
                        act.wait_ge(s_x3t, due(c, KD, k + 1))
                        A(x3T[0][:, k, :, :], graphs(6 + k), ACT.Copy).then_inc(s_x3hi, 1)
                if b is not None:
                    for half in range(2):
                        act.wait_ge(s_hp, due(b, 2, half + 1))
                        A(hexp[:, 2 * half:2 * half + 2, :], halves(4 + half), ACT.Exp).then_inc(s_hexp, 1)
                if c is not None:
                    for half in range(2):
                        act.wait_ge(s_z, due(c, 2, half + 1))
                        A(z[:, 2 * half:2 * half + 2, :], halves(6 + half), ACT.Copy).then_inc(s_zcp, 1)
                if t is not None:
                    act.wait_ge(s_lnrs[3], due(t, 1, 1))
                    norm_apply(3, v3, v3, s_x4)
                if b is not None:
                    act.wait_ge(s_lnrs[1], due(b, 1, 1))
                    norm_apply(1, x2[:, 1 - p, :, :], v1, s_x2)
                if c is not None:
                    for g in range(G):
                        act.wait_ge(s_uv, due(c, G, g + 1))
                        A(vals[:, g, :], ps[:, UV_BANK[g], D:2 * D], ACT.Copy).then_inc(s_v, 1)
                if a is not None:
                    act.wait_ge(s_lnrs[0], due(a, 1, 1))
                    norm_apply(0, x1[:, p, :, :], v0, s_x1)

            schedule(act, phase, middle, rest)

        @block.gpsimd
        def _(pool):
            P = nc.gpsimd
            P.memset(ident[:], 0.0)
            pool.drain()
            P.affine_select(out=ident[:], in_=ident[:], compare_op=ALU.not_equal, fill=1.0, base=0,
                            pattern=[[-1, N]], channel_multiplier=1).then_inc(s_ident, 1)
            pool.wait_ge(s_w1in, 16 * 3)
            P.tensor_scalar(b2_half[:], b2_row[:], 0.5, None, ALU.mult)
            pool.drain()

            def spread(col, n):
                return col.unsqueeze(2).to_broadcast([N, G, n])

            def norm_scale(layer, g):
                pool.wait_ge(s_lnst[layer], due(g, 1, 1))
                if layer in SHORT:
                    P.tensor_tensor(vare[:, layer, :], mv[:, layer, :, 1], eps[:], ALU.add)
                    P.tensor_scalar(nmean[:, layer, :], mv[:, layer, :, 0], -1.0, None, ALU.mult)
                    pool.drain()
                P.tensor_tensor(rstd[:, layer, :], vare[:, layer, :], neg_half[:], ALU.pow)
                pool.drain()
                P.tensor_tensor(nmr[:, layer, :], nmean[:, layer, :], rstd[:, layer, :], ALU.mult
                                ).then_inc(s_lnrs[layer], 1)

            def middle():
                pool.wait_ge(s_nodes, 16 * 2)
                P.tensor_scalar(no_loop[:], diag[:], 0.0, None, ALU.is_equal)
                pool.drain()

            def phase(p, f, a, b, c, t):
                if a is not None:
                    before(pool, s_v0, a, 2)
                    for g in range(G):
                        last = P.tensor_tensor(xb[:, g, :], x_sb[:, p, g, :], b2_half[:], ALU.add)
                    last.then_inc(s_xb, 1)
                if f is not None:
                    pool.wait_ge(s_Dinv, due(f, 1, 1))
                    P.tensor_tensor(H[:], H[:], spread(Dinv[:], N), ALU.mult).then_inc(s_HD, 1)
                    pool.wait_ge(s_HT, due(f, 1, 1))
                    P.tensor_tensor(HTB[:], HT[:], spread(Binv[:], N), ALU.mult).then_inc(s_HTB, 1)
                if c is not None:
                    for half in range(2):
                        gs = slice(2 * half, 2 * half + 2)
                        pool.wait_ge(s_th, due(c, 2, half + 1))
                        P.tensor_tensor(v2[:, gs, :], v2[:, gs, :], x2[:, p, gs, :], ALU.add).then_inc(s_v2, 1)
                    norm_scale(2, c)
                if a is not None:
                    pool.wait_ge(s_sq, due(a, KH, 2))
                    P.tensor_tensor(sqsum[:, 0, :, :], sq[:, 0, :, :], sq[:, 1, :, :], ALU.add)
                    pool.wait_ge(s_sq, due(a, KH, 4))
                    P.tensor_tensor(sqsum[:, 1, :, :], sq[:, 2, :, :], sq[:, 3, :, :], ALU.add)
                    pool.drain()
                    P.tensor_tensor(sqsum[:, 0, :, :], sqsum[:, 0, :, :], sqsum[:, 1, :, :], ALU.add).then_inc(s_sqsum, 1)
                if t is not None:
                    pool.wait_ge(s_pv, due(t, 1, 1))
                    P.tensor_tensor(v3[:], v3[:], x3[:, 1 - p, :, :], ALU.add).then_inc(s_v3, 1)
                    norm_scale(3, t)
                if a is not None:
                    pool.wait_ge(s_hvar, due(a, 1, 1))
                    P.tensor_tensor(hrstd[:], hvare[:], neg_half[:], ALU.pow).then_inc(s_hrstd, 1)
                    if c is not None:
                        pool.wait_ge(s_z, due(c, 2, 2))
                    P.tensor_tensor(adjTm[:, p, :, :], adjT[:, p, :, :], spread(nmask[:, bass.ds(a * G, G)], N), ALU.mult
                                    ).then_inc(s_adjTm, 1)
                    if c is not None:
                        pool.wait_ge(s_aggb, due(c, 2, 2))
                    pool.wait_ge(s_AT, due(a, 1, 1))
                    P.tensor_tensor(deg[:], rowsum[:, p, :], no_loop[:, bass.ds(a * G, G)], ALU.add)
                    pool.drain()
                    P.tensor_tensor(dinv[:, p, :], deg[:], neg_half[:], ALU.pow)
                    pool.drain()
                    P.tensor_tensor(ATd[:, p, :, :], AT[:], spread(dinv[:, p, :], N), ALU.mult).then_inc(s_ATd, 1)
                if b is not None:
                    norm_scale(1, b)
                if a is not None:
                    norm_scale(0, a)
                if c is not None:
                    pool.wait_ge(s_uz, due(c, G, G))
                    P.tensor_tensor(wcol[:], wraw[:], smask[:, bass.ds(c * G, G)], ALU.mult).then_inc(s_wcol, 1)

            schedule(pool, phase, middle)


def kernel(**inputs):
    import numpy as np
    import concourse.bacc as bacc
    from concourse.bass_utils import run_bass_kernel_spmd

    def plain(name):
        return np.ascontiguousarray(inputs[name])

    def turned(name):
        return np.ascontiguousarray(np.asarray(inputs[name]).T)

    def columns(name):
        return np.ascontiguousarray(np.asarray(inputs[name]).reshape(-1, 128).T)

    arrays = {
        "x": plain("x"), "adj": plain("adj"), "nodemask_t": turned("nodemask"),
        "w1_t": turned("L0_gnn_W1"), "b1_cols": columns("L0_gnn_b1"), "gamma_cols": columns("L0_gnn_gamma"),
        "beta_cols": columns("L0_gnn_beta"), "w2_t": turned("L0_gnn_W2"), "b2": plain("L0_gnn_b2"),
        "gat_w": plain("L1_gnn_W"), "gat_w_t": turned("L1_gnn_W"), "gat_a_cols": columns("L1_gnn_a"),
        "gcn_w": plain("L2_gnn_W"), "gcn_b": plain("L2_gnn_b"),
        "wqk_t": turned("L3_gnn_Wqk"), "wv": plain("L3_gnn_Wv"),
    }
    nc = bacc.Bacc("TRN2", target_bir_lowering=False, num_devices=1)
    arrays = {f"in_{name}": a for name, a in arrays.items()}
    args = [nc.dram_tensor(name, a.shape, mybir.dt.from_np(a.dtype), kind="ExternalInput").ap()
            for name, a in arrays.items()]
    out = nc.dram_tensor("out_x", inputs["x"].shape, mybir.dt.float32, kind="ExternalOutput").ap()
    gnn_stack_kernel(nc, *args, out)
    return run_bass_kernel_spmd(nc, [arrays], core_ids=[0]).results[0]["out_x"]
```
